# Optimizing a Trainium2 kernel written in Bass

```python
import numpy as np
import jax
import jax.numpy as jnp

def _softmax(x, axis=-1):
    return jax.nn.softmax(x, axis=axis)

def _gelu(x):
    return jax.nn.gelu(x, approximate=True)

def _silu(x):
    return jax.nn.silu(x)

def _sigmoid(x):
    return jax.nn.sigmoid(x)

def _layernorm(x, axis=-1, eps=1e-05):
    m = jnp.mean(x, axis=axis, keepdims=True)
    v = jnp.var(x, axis=axis, keepdims=True)
    return (x - m) / jnp.sqrt(v + eps)

def _scatter_add(tgt, idx, src, axis=0):
    return tgt.at[idx].add(src)

def _segment_sum(src, seg, n):
    return jax.ops.segment_sum(src, seg, n)
kernel_name = 'mk_dlrm_tower_d1_rec_r8_a90eeb'

def setup_inputs(seed: int=0):
    np.random.seed(seed)
    _w = jnp.asarray

    def _rec_inputs():
        import jax
        import jax.numpy as jnp
        _tk = jax.random.key(seed)
        dense_ctx = jax.random.normal(jax.random.fold_in(_tk, 190), (512, 16), jnp.float32)
        ids = jnp.stack([jax.random.randint(jax.random.fold_in(_tk, 200 + f), (512,), 0, v, jnp.int32) for f, v in enumerate([1000, 1250, 125000, 12500, 1250, 1250, 1250, 12500, 125000, 1000, 12500, 1250, 12500, 12500, 125000, 125000, 12500, 1250, 125000, 1250, 1250, 1000, 12500, 125000, 1250, 1000, 12500, 1000, 12500, 12500, 125000, 1000, 12500, 125000, 12500, 1250, 125000, 1250, 12500, 1000, 12500, 1250, 1000, 125000, 125000, 1000, 125000, 1250, 1250, 1000, 1000, 125000, 1250, 1000, 1000, 1250, 125000, 1000, 1000, 1000, 1000, 1000, 1250, 1250])], axis=1)
        tbl_0 = 0.05 * jax.random.normal(jax.random.fold_in(_tk, 500 + 0), (1000, 16), jnp.float32)
        tbl_1 = 0.05 * jax.random.normal(jax.random.fold_in(_tk, 500 + 1), (1250, 16), jnp.float32)
        tbl_2 = 0.05 * jax.random.normal(jax.random.fold_in(_tk, 500 + 2), (125000, 16), jnp.float32)
        tbl_3 = 0.05 * jax.random.normal(jax.random.fold_in(_tk, 500 + 3), (12500, 16), jnp.float32)
        tbl_4 = 0.05 * jax.random.normal(jax.random.fold_in(_tk, 500 + 4), (1250, 16), jnp.float32)
        tbl_5 = 0.05 * jax.random.normal(jax.random.fold_in(_tk, 500 + 5), (1250, 16), jnp.float32)
        tbl_6 = 0.05 * jax.random.normal(jax.random.fold_in(_tk, 500 + 6), (1250, 16), jnp.float32)
        tbl_7 = 0.05 * jax.random.normal(jax.random.fold_in(_tk, 500 + 7), (12500, 16), jnp.float32)
        tbl_8 = 0.05 * jax.random.normal(jax.random.fold_in(_tk, 500 + 8), (125000, 16), jnp.float32)
        tbl_9 = 0.05 * jax.random.normal(jax.random.fold_in(_tk, 500 + 9), (1000, 16), jnp.float32)
        tbl_10 = 0.05 * jax.random.normal(jax.random.fold_in(_tk, 500 + 10), (12500, 16), jnp.float32)
        tbl_11 = 0.05 * jax.random.normal(jax.random.fold_in(_tk, 500 + 11), (1250, 16), jnp.float32)
        tbl_12 = 0.05 * jax.random.normal(jax.random.fold_in(_tk, 500 + 12), (12500, 16), jnp.float32)
        tbl_13 = 0.05 * jax.random.normal(jax.random.fold_in(_tk, 500 + 13), (12500, 16), jnp.float32)
        tbl_14 = 0.05 * jax.random.normal(jax.random.fold_in(_tk, 500 + 14), (125000, 16), jnp.float32)
        tbl_15 = 0.05 * jax.random.normal(jax.random.fold_in(_tk, 500 + 15), (125000, 16), jnp.float32)
        tbl_16 = 0.05 * jax.random.normal(jax.random.fold_in(_tk, 500 + 16), (12500, 16), jnp.float32)
        tbl_17 = 0.05 * jax.random.normal(jax.random.fold_in(_tk, 500 + 17), (1250, 16), jnp.float32)
        tbl_18 = 0.05 * jax.random.normal(jax.random.fold_in(_tk, 500 + 18), (125000, 16), jnp.float32)
        tbl_19 = 0.05 * jax.random.normal(jax.random.fold_in(_tk, 500 + 19), (1250, 16), jnp.float32)
        tbl_20 = 0.05 * jax.random.normal(jax.random.fold_in(_tk, 500 + 20), (1250, 16), jnp.float32)
        tbl_21 = 0.05 * jax.random.normal(jax.random.fold_in(_tk, 500 + 21), (1000, 16), jnp.float32)
        tbl_22 = 0.05 * jax.random.normal(jax.random.fold_in(_tk, 500 + 22), (12500, 16), jnp.float32)
        tbl_23 = 0.05 * jax.random.normal(jax.random.fold_in(_tk, 500 + 23), (125000, 16), jnp.float32)
        tbl_24 = 0.05 * jax.random.normal(jax.random.fold_in(_tk, 500 + 24), (1250, 16), jnp.float32)
        tbl_25 = 0.05 * jax.random.normal(jax.random.fold_in(_tk, 500 + 25), (1000, 16), jnp.float32)
        tbl_26 = 0.05 * jax.random.normal(jax.random.fold_in(_tk, 500 + 26), (12500, 16), jnp.float32)
        tbl_27 = 0.05 * jax.random.normal(jax.random.fold_in(_tk, 500 + 27), (1000, 16), jnp.float32)
        tbl_28 = 0.05 * jax.random.normal(jax.random.fold_in(_tk, 500 + 28), (12500, 16), jnp.float32)
        tbl_29 = 0.05 * jax.random.normal(jax.random.fold_in(_tk, 500 + 29), (12500, 16), jnp.float32)
        tbl_30 = 0.05 * jax.random.normal(jax.random.fold_in(_tk, 500 + 30), (125000, 16), jnp.float32)
        tbl_31 = 0.05 * jax.random.normal(jax.random.fold_in(_tk, 500 + 31), (1000, 16), jnp.float32)
        tbl_32 = 0.05 * jax.random.normal(jax.random.fold_in(_tk, 500 + 32), (12500, 16), jnp.float32)
        tbl_33 = 0.05 * jax.random.normal(jax.random.fold_in(_tk, 500 + 33), (125000, 16), jnp.float32)
        tbl_34 = 0.05 * jax.random.normal(jax.random.fold_in(_tk, 500 + 34), (12500, 16), jnp.float32)
        tbl_35 = 0.05 * jax.random.normal(jax.random.fold_in(_tk, 500 + 35), (1250, 16), jnp.float32)
        tbl_36 = 0.05 * jax.random.normal(jax.random.fold_in(_tk, 500 + 36), (125000, 16), jnp.float32)
        tbl_37 = 0.05 * jax.random.normal(jax.random.fold_in(_tk, 500 + 37), (1250, 16), jnp.float32)
        tbl_38 = 0.05 * jax.random.normal(jax.random.fold_in(_tk, 500 + 38), (12500, 16), jnp.float32)
        tbl_39 = 0.05 * jax.random.normal(jax.random.fold_in(_tk, 500 + 39), (1000, 16), jnp.float32)
        tbl_40 = 0.05 * jax.random.normal(jax.random.fold_in(_tk, 500 + 40), (12500, 16), jnp.float32)
        tbl_41 = 0.05 * jax.random.normal(jax.random.fold_in(_tk, 500 + 41), (1250, 16), jnp.float32)
        tbl_42 = 0.05 * jax.random.normal(jax.random.fold_in(_tk, 500 + 42), (1000, 16), jnp.float32)
        tbl_43 = 0.05 * jax.random.normal(jax.random.fold_in(_tk, 500 + 43), (125000, 16), jnp.float32)
        tbl_44 = 0.05 * jax.random.normal(jax.random.fold_in(_tk, 500 + 44), (125000, 16), jnp.float32)
        tbl_45 = 0.05 * jax.random.normal(jax.random.fold_in(_tk, 500 + 45), (1000, 16), jnp.float32)
        tbl_46 = 0.05 * jax.random.normal(jax.random.fold_in(_tk, 500 + 46), (125000, 16), jnp.float32)
        tbl_47 = 0.05 * jax.random.normal(jax.random.fold_in(_tk, 500 + 47), (1250, 16), jnp.float32)
        tbl_48 = 0.05 * jax.random.normal(jax.random.fold_in(_tk, 500 + 48), (1250, 16), jnp.float32)
        tbl_49 = 0.05 * jax.random.normal(jax.random.fold_in(_tk, 500 + 49), (1000, 16), jnp.float32)
        tbl_50 = 0.05 * jax.random.normal(jax.random.fold_in(_tk, 500 + 50), (1000, 16), jnp.float32)
        tbl_51 = 0.05 * jax.random.normal(jax.random.fold_in(_tk, 500 + 51), (125000, 16), jnp.float32)
        tbl_52 = 0.05 * jax.random.normal(jax.random.fold_in(_tk, 500 + 52), (1250, 16), jnp.float32)
        tbl_53 = 0.05 * jax.random.normal(jax.random.fold_in(_tk, 500 + 53), (1000, 16), jnp.float32)
        tbl_54 = 0.05 * jax.random.normal(jax.random.fold_in(_tk, 500 + 54), (1000, 16), jnp.float32)
        tbl_55 = 0.05 * jax.random.normal(jax.random.fold_in(_tk, 500 + 55), (1250, 16), jnp.float32)
        tbl_56 = 0.05 * jax.random.normal(jax.random.fold_in(_tk, 500 + 56), (125000, 16), jnp.float32)
        tbl_57 = 0.05 * jax.random.normal(jax.random.fold_in(_tk, 500 + 57), (1000, 16), jnp.float32)
        tbl_58 = 0.05 * jax.random.normal(jax.random.fold_in(_tk, 500 + 58), (1000, 16), jnp.float32)
        tbl_59 = 0.05 * jax.random.normal(jax.random.fold_in(_tk, 500 + 59), (1000, 16), jnp.float32)
        tbl_60 = 0.05 * jax.random.normal(jax.random.fold_in(_tk, 500 + 60), (1000, 16), jnp.float32)
        tbl_61 = 0.05 * jax.random.normal(jax.random.fold_in(_tk, 500 + 61), (1000, 16), jnp.float32)
        tbl_62 = 0.05 * jax.random.normal(jax.random.fold_in(_tk, 500 + 62), (1250, 16), jnp.float32)
        tbl_63 = 0.05 * jax.random.normal(jax.random.fold_in(_tk, 500 + 63), (1250, 16), jnp.float32)
        _rk = jax.random.fold_in(_tk, 7)
        W_top1 = 0.05 * jax.random.normal(jax.random.fold_in(_tk, 801), (400, 512), jnp.float32)
        W_top2 = 0.0441942 * jax.random.normal(jax.random.fold_in(_tk, 802), (512, 256), jnp.float32)
        W_top3 = 0.0625 * jax.random.normal(jax.random.fold_in(_tk, 803), (256, 1), jnp.float32)
        b_top1 = jnp.zeros((512,), jnp.float32)
        b_top2 = jnp.zeros((256,), jnp.float32)
        return (dense_ctx, ids, tbl_0, tbl_1, tbl_2, tbl_3, tbl_4, tbl_5, tbl_6, tbl_7, tbl_8, tbl_9, tbl_10, tbl_11, tbl_12, tbl_13, tbl_14, tbl_15, tbl_16, tbl_17, tbl_18, tbl_19, tbl_20, tbl_21, tbl_22, tbl_23, tbl_24, tbl_25, tbl_26, tbl_27, tbl_28, tbl_29, tbl_30, tbl_31, tbl_32, tbl_33, tbl_34, tbl_35, tbl_36, tbl_37, tbl_38, tbl_39, tbl_40, tbl_41, tbl_42, tbl_43, tbl_44, tbl_45, tbl_46, tbl_47, tbl_48, tbl_49, tbl_50, tbl_51, tbl_52, tbl_53, tbl_54, tbl_55, tbl_56, tbl_57, tbl_58, tbl_59, tbl_60, tbl_61, tbl_62, tbl_63, W_top1, b_top1, W_top2, b_top2, W_top3)
    dense_ctx, ids, tbl_0, tbl_1, tbl_2, tbl_3, tbl_4, tbl_5, tbl_6, tbl_7, tbl_8, tbl_9, tbl_10, tbl_11, tbl_12, tbl_13, tbl_14, tbl_15, tbl_16, tbl_17, tbl_18, tbl_19, tbl_20, tbl_21, tbl_22, tbl_23, tbl_24, tbl_25, tbl_26, tbl_27, tbl_28, tbl_29, tbl_30, tbl_31, tbl_32, tbl_33, tbl_34, tbl_35, tbl_36, tbl_37, tbl_38, tbl_39, tbl_40, tbl_41, tbl_42, tbl_43, tbl_44, tbl_45, tbl_46, tbl_47, tbl_48, tbl_49, tbl_50, tbl_51, tbl_52, tbl_53, tbl_54, tbl_55, tbl_56, tbl_57, tbl_58, tbl_59, tbl_60, tbl_61, tbl_62, tbl_63, W_top1, b_top1, W_top2, b_top2, W_top3 = _rec_inputs()

    def _L0_rec_setup():
        import jax, jax.numpy as jnp
        import numpy as np
        B, F0, D = (256, 64, 16)
        CIN_SIZES = [128, 128, 128]

        def _cin_layer(x0, xi, W):
            F0_, Fi, Fn = (x0.shape[1], xi.shape[1], W.shape[-1])
            Wr = W.reshape(F0_, Fi, Fn)
            return jnp.einsum('bid,bjd,ijn->bnd', x0, xi, Wr)
        key = jax.random.key(seed)
        ks = jax.random.split(key, 4)
        x = jax.random.normal(ks[0], (B, F0, D), dtype=jnp.float32)
        field_nums = [F0] + CIN_SIZES
        Ws = []
        for i in range(len(CIN_SIZES)):
            fan_in = F0 * field_nums[i]
            fan_out = field_nums[i + 1]
            limit = np.sqrt(6.0 / (fan_in + fan_out)).astype(np.float32)
            W = jax.random.uniform(ks[i + 1], (fan_in, fan_out), dtype=jnp.float32, minval=-limit, maxval=limit)
            Ws.append(W)
        return {'x': x, 'W0': Ws[0], 'W1': Ws[1], 'W2': Ws[2]}
    _L0_rec_all = _L0_rec_setup()
    _L0_rec_in = {k: v for k, v in _L0_rec_all.items() if k in ('W0', 'W1', 'W2')}
    del _L0_rec_all
    return {'dense_ctx': dense_ctx, 'ids': ids, 'tbl_0': tbl_0, 'tbl_1': tbl_1, 'tbl_2': tbl_2, 'tbl_3': tbl_3, 'tbl_4': tbl_4, 'tbl_5': tbl_5, 'tbl_6': tbl_6, 'tbl_7': tbl_7, 'tbl_8': tbl_8, 'tbl_9': tbl_9, 'tbl_10': tbl_10, 'tbl_11': tbl_11, 'tbl_12': tbl_12, 'tbl_13': tbl_13, 'tbl_14': tbl_14, 'tbl_15': tbl_15, 'tbl_16': tbl_16, 'tbl_17': tbl_17, 'tbl_18': tbl_18, 'tbl_19': tbl_19, 'tbl_20': tbl_20, 'tbl_21': tbl_21, 'tbl_22': tbl_22, 'tbl_23': tbl_23, 'tbl_24': tbl_24, 'tbl_25': tbl_25, 'tbl_26': tbl_26, 'tbl_27': tbl_27, 'tbl_28': tbl_28, 'tbl_29': tbl_29, 'tbl_30': tbl_30, 'tbl_31': tbl_31, 'tbl_32': tbl_32, 'tbl_33': tbl_33, 'tbl_34': tbl_34, 'tbl_35': tbl_35, 'tbl_36': tbl_36, 'tbl_37': tbl_37, 'tbl_38': tbl_38, 'tbl_39': tbl_39, 'tbl_40': tbl_40, 'tbl_41': tbl_41, 'tbl_42': tbl_42, 'tbl_43': tbl_43, 'tbl_44': tbl_44, 'tbl_45': tbl_45, 'tbl_46': tbl_46, 'tbl_47': tbl_47, 'tbl_48': tbl_48, 'tbl_49': tbl_49, 'tbl_50': tbl_50, 'tbl_51': tbl_51, 'tbl_52': tbl_52, 'tbl_53': tbl_53, 'tbl_54': tbl_54, 'tbl_55': tbl_55, 'tbl_56': tbl_56, 'tbl_57': tbl_57, 'tbl_58': tbl_58, 'tbl_59': tbl_59, 'tbl_60': tbl_60, 'tbl_61': tbl_61, 'tbl_62': tbl_62, 'tbl_63': tbl_63, 'W_top1': W_top1, 'b_top1': b_top1, 'W_top2': W_top2, 'b_top2': b_top2, 'W_top3': W_top3, 'L0_rec_W0': _L0_rec_in['W0'], 'L0_rec_W1': _L0_rec_in['W1'], 'L0_rec_W2': _L0_rec_in['W2']}

def reference(dense_ctx, ids, tbl_0, tbl_1, tbl_2, tbl_3, tbl_4, tbl_5, tbl_6, tbl_7, tbl_8, tbl_9, tbl_10, tbl_11, tbl_12, tbl_13, tbl_14, tbl_15, tbl_16, tbl_17, tbl_18, tbl_19, tbl_20, tbl_21, tbl_22, tbl_23, tbl_24, tbl_25, tbl_26, tbl_27, tbl_28, tbl_29, tbl_30, tbl_31, tbl_32, tbl_33, tbl_34, tbl_35, tbl_36, tbl_37, tbl_38, tbl_39, tbl_40, tbl_41, tbl_42, tbl_43, tbl_44, tbl_45, tbl_46, tbl_47, tbl_48, tbl_49, tbl_50, tbl_51, tbl_52, tbl_53, tbl_54, tbl_55, tbl_56, tbl_57, tbl_58, tbl_59, tbl_60, tbl_61, tbl_62, tbl_63, W_top1, b_top1, W_top2, b_top2, W_top3, L0_rec_W0, L0_rec_W1, L0_rec_W2):
    import jax
    import jax.numpy as jnp

    def _L0_rec_ref(x, W0, W1, W2):
        import jax, jax.numpy as jnp
        import numpy as np
        B, F0, D = (256, 64, 16)
        CIN_SIZES = [128, 128, 128]

        def _cin_layer(x0, xi, W):
            F0_, Fi, Fn = (x0.shape[1], xi.shape[1], W.shape[-1])
            Wr = W.reshape(F0_, Fi, Fn)
            return jnp.einsum('bid,bjd,ijn->bnd', x0, xi, Wr)
        h = x
        outs = []
        for W in (W0, W1, W2):
            h = _cin_layer(x, h, W)
            outs.append(h)
        res = jnp.concatenate(outs, axis=1)
        return jnp.sum(res, axis=-1)
    e = jnp.stack([tbl_0[ids[:, 0]], tbl_1[ids[:, 1]], tbl_2[ids[:, 2]], tbl_3[ids[:, 3]], tbl_4[ids[:, 4]], tbl_5[ids[:, 5]], tbl_6[ids[:, 6]], tbl_7[ids[:, 7]], tbl_8[ids[:, 8]], tbl_9[ids[:, 9]], tbl_10[ids[:, 10]], tbl_11[ids[:, 11]], tbl_12[ids[:, 12]], tbl_13[ids[:, 13]], tbl_14[ids[:, 14]], tbl_15[ids[:, 15]], tbl_16[ids[:, 16]], tbl_17[ids[:, 17]], tbl_18[ids[:, 18]], tbl_19[ids[:, 19]], tbl_20[ids[:, 20]], tbl_21[ids[:, 21]], tbl_22[ids[:, 22]], tbl_23[ids[:, 23]], tbl_24[ids[:, 24]], tbl_25[ids[:, 25]], tbl_26[ids[:, 26]], tbl_27[ids[:, 27]], tbl_28[ids[:, 28]], tbl_29[ids[:, 29]], tbl_30[ids[:, 30]], tbl_31[ids[:, 31]], tbl_32[ids[:, 32]], tbl_33[ids[:, 33]], tbl_34[ids[:, 34]], tbl_35[ids[:, 35]], tbl_36[ids[:, 36]], tbl_37[ids[:, 37]], tbl_38[ids[:, 38]], tbl_39[ids[:, 39]], tbl_40[ids[:, 40]], tbl_41[ids[:, 41]], tbl_42[ids[:, 42]], tbl_43[ids[:, 43]], tbl_44[ids[:, 44]], tbl_45[ids[:, 45]], tbl_46[ids[:, 46]], tbl_47[ids[:, 47]], tbl_48[ids[:, 48]], tbl_49[ids[:, 49]], tbl_50[ids[:, 50]], tbl_51[ids[:, 51]], tbl_52[ids[:, 52]], tbl_53[ids[:, 53]], tbl_54[ids[:, 54]], tbl_55[ids[:, 55]], tbl_56[ids[:, 56]], tbl_57[ids[:, 57]], tbl_58[ids[:, 58]], tbl_59[ids[:, 59]], tbl_60[ids[:, 60]], tbl_61[ids[:, 61]], tbl_62[ids[:, 62]], tbl_63[ids[:, 63]]], axis=1)
    z = _L0_rec_ref(e, L0_rec_W0, L0_rec_W1, L0_rec_W2)
    z = z.reshape(z.shape[0], -1)
    h = jnp.concatenate([z, dense_ctx], axis=1)
    h = jnp.maximum(h @ W_top1 + b_top1, 0.0)
    h = jnp.maximum(h @ W_top2 + b_top2, 0.0)
    y = h @ W_top3
    return y

_drawn_inputs = setup_inputs


def setup_inputs(seed=0):
    import zlib

    import numpy as np

    out = dict(_drawn_inputs(seed))
    spreads = {'b_top1': (0.0, 0.783), 'b_top2': (0.0, 0.354)}
    factors = {'tbl_0': 8.0,
     'tbl_1': 8.0,
     'tbl_2': 8.0,
     'tbl_3': 8.0,
     'tbl_4': 8.0,
     'tbl_5': 8.0,
     'tbl_6': 8.0,
     'tbl_7': 8.0,
     'tbl_8': 8.0,
     'tbl_9': 8.0,
     'tbl_10': 8.0,
     'tbl_11': 8.0,
     'tbl_12': 8.0,
     'tbl_13': 8.0,
     'tbl_14': 8.0,
     'tbl_15': 8.0,
     'tbl_16': 8.0,
     'tbl_17': 8.0,
     'tbl_18': 8.0,
     'tbl_19': 8.0,
     'tbl_20': 8.0,
     'tbl_21': 8.0,
     'tbl_22': 8.0,
     'tbl_23': 8.0,
     'tbl_24': 7.938,
     'tbl_25': 8.0,
     'tbl_26': 8.0,
     'tbl_27': 8.0,
     'tbl_28': 8.0,
     'tbl_29': 8.0,
     'tbl_30': 8.0,
     'tbl_31': 8.0,
     'tbl_32': 8.0,
     'tbl_33': 8.0,
     'tbl_34': 8.0,
     'tbl_35': 8.0,
     'tbl_36': 8.0,
     'tbl_37': 8.0,
     'tbl_38': 7.688,
     'tbl_39': 8.0,
     'tbl_40': 8.0,
     'tbl_41': 8.0,
     'tbl_42': 8.0,
     'tbl_43': 7.977,
     'tbl_44': 8.0,
     'tbl_45': 8.0,
     'tbl_46': 8.0,
     'tbl_47': 8.0,
     'tbl_48': 8.0,
     'tbl_49': 8.0,
     'tbl_50': 8.0,
     'tbl_51': 8.0,
     'tbl_52': 8.0,
     'tbl_53': 8.0,
     'tbl_54': 8.0,
     'tbl_55': 8.0,
     'tbl_56': 8.0,
     'tbl_57': 8.0,
     'tbl_58': 8.0,
     'tbl_59': 8.0,
     'tbl_60': 8.0,
     'tbl_61': 8.0,
     'tbl_62': 8.0,
     'tbl_63': 8.0,
     'L0_rec_W1': 8.0,
     'L0_rec_W2': 8.0}
    for name, (base, spread) in spreads.items():
        noise = np.random.default_rng([zlib.crc32(name.encode()), seed]).standard_normal(out[name].shape)
        drawn = base * np.exp(spread * noise) if base else spread * noise
        out[name] = jnp.asarray(drawn.astype(out[name].dtype))
    for name, factor in factors.items():
        out[name] = (out[name] * factor).astype(out[name].dtype)
    return out
```

```python
from contextlib import ExitStack

import concourse.bass as bass
from concourse import mybir

F32 = mybir.dt.float32
I32 = mybir.dt.int32
U32 = mybir.dt.uint32
ALU = mybir.AluOpType
ACT = mybir.ActivationFunctionType
AX_X = mybir.AxisListType.X

P = 128
FIELDS, DIM, BATCH = 64, 16, 512
NF = 128
CH = 512
SAMPLES = CH // DIM
CHUNKS = BATCH * DIM // CH
PER_BLOCK = P // SAMPLES
BLOCKS = CHUNKS // PER_BLOCK
XA, RB = 8, 16
N_X = FIELDS // XA
N_Y = FIELDS // RB
N_H = NF // RB
PAIR = 2
SUB = CH // P
SUB_B = P // DIM
RING = 6
PROD = 4
W2_I, W2_SLOTS = 4, 4
HIDDEN1, HIDDEN2, DENSE = 512, 256, 16

LAYER1_EARLY = 6
L1_A = [(1, c, a, c) for c in range(LAYER1_EARLY) for a in range(0, N_X, PAIR)]
L0 = [(0, c, a, c) for c in range(N_Y) for a in range(0, 2 * c + 2, PAIR)]
L0_MID = [(l, c, a, j + LAYER1_EARLY) for l, c, a, j in L0]
L1_B = [(1, c, a, c + N_Y) for c in range(LAYER1_EARLY, N_H) for a in range(0, N_X, PAIR)]
GROUPS = L1_A + L0_MID + L1_B
GROUPS_LAST = L1_A + [(1, c, a, c) for c in range(LAYER1_EARLY, N_H) for a in range(0, N_X, PAIR)]
N_G, N_R = len(GROUPS), N_Y + N_H
L0_END = len(L1_A) + len(L0)
W0_TILES = [(c, a) for c in range(N_Y) for a in range(2 * c + 2)]

XCOL_AT = 0
XT_AT = (1, 2, 3, 4)
H2T_AT = 6
G_AT = (9, 12, 15, 18)
F_AT = 24
F_LOADS = FIELDS // W2_I


def first_of(groups, g):
    return g == 0 or groups[g - 1][3] != groups[g][3]


def groups_before(t, g):
    return t * N_G + (len(L0) + g)


def rhs_before(t, j):
    return t * N_R + (N_Y + j)


def prod_slot(q, g):
    return (len(L0) + N_G * (q + 1) + g) % PROD


def turns_before(bt, q):
    if q < 0:
        return 4
    return bt * 12 + (5 + 2 * q + (4 if q > 2 else 0))


def g_before(bt, q, s):
    return bt * 18 + (4 * q + s)


def build(nc, ins, out):
    with ExitStack() as ctx:
        def sb(name, shape, dt=F32):
            return ctx.enter_context(nc.sbuf_tensor(f"{name}_sb", shape, dt))

        def psum(name, shape):
            return ctx.enter_context(nc.psum_tensor(name, shape, F32))

        def sem(name):
            return ctx.enter_context(nc.semaphore(name))

        x_dram = nc.dram_tensor("x_scratch", [FIELDS, CHUNKS * CH], F32, kind="Internal").ap()
        h1_dram = nc.dram_tensor("h1_scratch", [NF, CHUNKS * CH], F32, kind="Internal").ap()

        ident = sb("ident", [P, P])
        mask = sb("mask", [P, SUB_B])
        w0 = sb("w0", [P, len(W0_TILES), NF])
        w1 = sb("w1", [P, N_H, N_X, NF])
        w2 = sb("w2", [P, W2_SLOTS, W2_I, NF])
        ids = sb("ids", [P, BLOCKS, FIELDS], I32)
        ids_now = sb("ids_now", [P, FIELDS], I32)
        rows = sb("rows", [P, FIELDS, DIM])
        xt = sb("xt", [FIELDS, P, DIM])
        x_tiles = sb("x_tiles", [P, 2, N_X, CH])
        rhs_ring = sb("rhs_ring", [P, RING, CH])
        prod = sb("prod", [P, PROD, PAIR, CH])
        h1 = sb("h1", [NF, CH])
        h2 = sb("h2", [NF, CH])
        h2t = sb("h2t", [P, SUB, NF])
        xcol = sb("xcol", [P, 2, SUB, FIELDS])
        xdiag = sb("xdiag", [P, 2, SUB_B, FIELDS])
        gsum = sb("gsum", [NF, FIELDS, P])
        z = sb("z", [NF, 3, BATCH])
        top = x_tiles[:, 0].rearrange("p a n -> p (a n)")
        wt1 = top[:, 0:4 * HIDDEN1].rearrange("p (k n) -> p k n", k=4)
        wt2 = top[:, 2048:2048 + 4 * HIDDEN2].rearrange("p (k n) -> p k n", k=4)
        wt3 = top[:, 3072:3072 + 2]
        bt1 = top[:, 3080:3084]
        bt2 = top[:, 3088:3090]
        dense = top[0:DENSE, 3584:3584 + BATCH]
        hid1 = x_tiles[:, 1, 0:4, :]
        hid2 = x_tiles[:, 1, 4:6, :]
        y = x_tiles[0:1, 1, 6, :]

        acc1 = psum("acc1", [P, 2, CH])
        acc0 = psum("acc0", [P, CH])
        rhs = psum("rhs", [P, 2, CH])
        turn = psum("turn", [P, CH])
        gbank = psum("gbank", [P, 2, CH])

        ids_loaded = sem("ids_loaded")
        consts_loaded = sem("consts_loaded")
        w0_loaded = sem("w0_loaded")
        w0_summed = sem("w0_summed")
        w1_loaded = [sem(f"w1_loaded{c}") for c in range(N_H)]
        w2_loaded = [sem(f"w2_loaded{k}") for k in range(W2_SLOTS)]
        w2_free = sem("w2_free")
        top_loaded = sem("top_loaded")
        ids_copied = sem("ids_copied")
        rows_gathered = sem("rows_gathered")
        x_stored = sem("x_stored")
        x_loaded = [sem(f"x_loaded{k}") for k in range(2)]
        rhs_loaded = [sem(f"rhs_loaded{k}") for k in range(RING)]
        rhs_ready = sem("rhs_ready")
        prod_ready = sem("prod_ready")
        prod_used = sem("prod_used")
        h1_copied = sem("h1_copied")
        h1_stored = sem("h1_stored")
        h2_copied = sem("h2_copied")
        turned = sem("turned")
        turn_copied = sem("turn_copied")
        xdiag_ready = sem("xdiag_ready")
        g_done = sem("g_done")
        g_free = sem("g_free")
        z_summed = sem("z_summed")
        hid_done = sem("hid_done")
        hid_copied = sem("hid_copied")
        y_stored = sem("y_stored")
        pe_passed = sem("pe_passed")
        pool_passed = sem("pool_passed")

        w0_view = ins["w0_tiles"]
        w1_view = ins["w1_tiles"]

        block = ctx.enter_context(nc.Block())

        def each_chunk(eng, chunk):
            chunk(0, -1, 0)
            with eng.Fori(0, BLOCKS - 1) as bt:
                for q in range(PER_BLOCK):
                    chunk(bt, q, bt * PER_BLOCK + (q + 1))
            for q in range(PER_BLOCK - 1):
                chunk(BLOCKS - 1, q, (BLOCKS - 1) * PER_BLOCK + q + 1)

        def is_last(t):
            return isinstance(t, int) and t == CHUNKS - 1

        def makes_xt(bt, q):
            return q == 2 and not (isinstance(bt, int) and bt == BLOCKS - 1)

        @block.sync
        def _(sp):
            def load_x(t, par, k):
                cols = bass.ds(t * CH, CH)
                for a in range(N_X):
                    src = x_dram[a * XA:(a + 1) * XA, cols].unsqueeze(1).to_broadcast([XA, RB, CH])
                    sp.dma_start(x_tiles[:, par, a, :], src).then_inc(x_loaded[par], 16)

            def load_rhs(n, src, wait):
                slot = wait[0]
                if wait[1] is not None:
                    sp.wait_ge(rhs_ready, wait[1])
                rep = src.unsqueeze(0).to_broadcast([XA, RB, CH])
                sp.dma_start(rhs_ring[:, slot, :], rep).then_inc(rhs_loaded[slot], 16)

            sp.dma_start(ids[:], ins["ids"].rearrange("(t p) f -> p t f", p=P)).then_inc(ids_loaded, 16)
            sp.dma_start(ident[:], ins["identity"]).then_inc(consts_loaded, 16)
            sp.dma_start(mask[:], ins["sample_mask"]).then_inc(consts_loaded, 16)
            sp.dma_start(w0[:], w0_view[0]).then_inc(w0_loaded, 16)
            w0_off = x_tiles[:, 1].rearrange("p a n -> p (a n)")[:, 0:len(W0_TILES) * NF]
            sp.dma_start(w0_off, w0_view[1].rearrange("p t n -> p (t n)")).then_inc(w0_loaded, 16)
            for c in range(N_H):
                sp.dma_start(w1[:, c], w1_view[:, c]).then_inc(w1_loaded[c], 16)

            sp.wait_ge(x_stored, 16)
            load_x(0, 0, 0)
            for c in range(N_Y):
                load_rhs(c, x_dram[c * RB:(c + 1) * RB, 0:CH], (c, None))

            def chunk(bt, q, t):
                last = is_last(t)
                now, nxt = bass.ds(t * CH, CH), bass.ds(t * CH + CH, CH)
                places = N_H if last else N_R

                def rhs_load(j):
                    slot = (N_Y + j) % RING
                    n = rhs_before(t, j)
                    before = n - (RING - 1)
                    wait = (slot, None if isinstance(n, int) and before <= 0 else before)
                    if not last and LAYER1_EARLY <= j < LAYER1_EARLY + N_Y:
                        c = j - LAYER1_EARLY
                        load_rhs(n, x_dram[c * RB:(c + 1) * RB, nxt], wait)
                    else:
                        c = j if j < LAYER1_EARLY or last else j - N_Y
                        load_rhs(n, h1_dram[c * RB:(c + 1) * RB, now], wait)

                sp.wait_ge(h1_stored, t * 16 + 16)
                for j in range(LAYER1_EARLY):
                    rhs_load(j)
                if not last:
                    sp.wait_ge(prod_ready, groups_before(t, 0))
                    if q < 0:
                        sp.wait_ge(w0_summed, 1)
                    if q == 2:
                        sp.wait_ge(x_stored, bt * 16 + 32)
                    load_x(t + 1, q % 2, 0)
                if last:
                    sp.wait_ge(prod_ready, groups_before(t, 0))
                    sp.dma_start(wt1[:, 0:3, :], ins["W_top1"][0:3 * P, :].rearrange("(k p) n -> p k n", p=P)).then_inc(top_loaded, 16)
                    sp.dma_start(wt1[0:DENSE, 3, :], ins["W_top1"][3 * P:3 * P + DENSE, :]).then_inc(top_loaded, 16)
                    sp.dma_start(wt2, ins["W_top2"].rearrange("(k p) n -> p k n", p=P)).then_inc(top_loaded, 16)
                    sp.dma_start(wt3, ins["w_top3_cols"]).then_inc(top_loaded, 16)
                    sp.dma_start(bt1, ins["b_top1_cols"]).then_inc(top_loaded, 16)
                    sp.dma_start(bt2, ins["b_top2_cols"]).then_inc(top_loaded, 16)
                    sp.dma_start(dense, ins["dense_rows"]).then_inc(top_loaded, 16)
                for j in range(LAYER1_EARLY, places):
                    rhs_load(j)
                if q == 3:
                    w2_loads(bt)

            def w2_loads(bt):
                for k in range(F_LOADS):
                    sp.wait_ge(w2_free, bt * F_LOADS + (k + 1))
                    sp.dma_start(w2[:, k % W2_SLOTS], ins["w2_rows"][:, k * W2_I:(k + 1) * W2_I, :]).then_inc(
                        w2_loaded[k % W2_SLOTS], 16)

            each_chunk(sp, chunk)
            w2_loads(BLOCKS - 1)
            sp.wait_ge(hid_copied, 7)
            sp.dma_start(out.rearrange("b o -> o b"), y).then_inc(y_stored, 16)
            sp.wait_ge(y_stored, 16)

        @block.gpsimd
        def _(pool):
            def gather(bt, half):
                if half == 0:
                    if not isinstance(bt, int):
                        pool.wait_ge(rows_gathered, bt * (16 * FIELDS))
                    pool.tensor_copy(ids_now[:], ids[:, bass.ds(bt, 1), :].rearrange("p o f -> p (o f)")).then_inc(ids_copied, 1)
                    pool.wait_ge(ids_copied, bt + 1)
                    pool.sem_inc(pool_passed, 1)
                for f in range(half * FIELDS // 2, (half + 1) * FIELDS // 2):
                    pool.indirect_dma_start(
                        rows[:, f, :], None, ins[f"tbl_{f}"],
                        bass.IndirectOffsetOnAxis(ap=ids_now[:, f:f + 1].bitcast(U32), axis=0),
                    ).then_inc(rows_gathered, 16)

            def diagonal(bt, q):
                for s in range(SUB):
                    pool.wait_ge(g_free, g_before(bt, q, s) + 1)
                    src = xcol[:, q % 2, s, :].unsqueeze(1).to_broadcast([P, SUB_B, FIELDS])
                    on = mask[:].unsqueeze(2).to_broadcast([P, SUB_B, FIELDS])
                    pool.tensor_tensor(xdiag[:, s % 2], src, on, ALU.mult).then_inc(xdiag_ready, 1)

            def chunk(bt, q, t):
                if q < 0:
                    return
                pool.wait_ge(turn_copied, turns_before(bt, q) if q < 3 or not isinstance(bt, int) else turns_before(bt, 2) + 2)
                diagonal(bt, q)
                if q < 2 and not isinstance(bt, int):
                    gather(bt + 1, q)

            pool.wait_ge(ids_loaded, 16)
            gather(0, 0)
            gather(0, 1)
            pool.wait_ge(consts_loaded, 32)
            each_chunk(pool, chunk)
            chunk(BLOCKS - 1, PER_BLOCK - 1, CHUNKS)

        @block.vector
        def _(dve):
            dve.wait_ge(w0_loaded, 32)
            w0_flat = w0[:].rearrange("p t n -> p (t n)")
            w0_off = x_tiles[:, 1].rearrange("p a n -> p (a n)")[:, 0:len(W0_TILES) * NF]
            dve.tensor_tensor(w0_flat, w0_flat, w0_off, ALU.add).then_inc(w0_summed, 1)

            def product(n, slot, bank, par, a, x_n=None, rhs_n=None):
                if rhs_n is not None:
                    dve.wait_ge(rhs_ready, rhs_n)
                if x_n is not None:
                    dve.wait_ge(x_loaded[par], x_n)
                if not isinstance(n, int) or n >= PROD:
                    dve.wait_ge(prod_used, n - (PROD - 1))
                dve.tensor_tensor(
                    prod[:, slot], x_tiles[:, par, a:a + PAIR, :],
                    rhs[:, bank:bank + 1, :].to_broadcast([P, PAIR, CH]), ALU.mult,
                ).then_inc(prod_ready, 1)

            def sum_over_d(layer, src, t):
                dve.tensor_reduce(
                    z[:, layer, bass.ds(t * SAMPLES, SAMPLES)], src[:].rearrange("p (b d) -> p b d", d=DIM),
                    AX_X, ALU.add).then_inc(z_summed, 1)

            for g, (_, c, a, j) in enumerate(L0):
                product(g, g % PROD, j % 2, 0, a, 16 * N_X if g == 0 else None,
                        j + 1 if first_of(L0, g) else None)
            dve.wait_ge(h1_copied, 1)
            sum_over_d(0, h1, 0)

            def chunk(bt, q, t):
                last = is_last(t)
                groups = GROUPS_LAST if last else GROUPS
                for g, (layer, c, a, j) in enumerate(groups):
                    if g == 8 and q >= 0:
                        dve.wait_ge(h2_copied, t)
                        sum_over_d(1, h2, t - 1)
                    if g == L0_END + 3 and not last:
                        dve.wait_ge(h1_copied, t + 2)
                        sum_over_d(0, h1, t + 1)
                    par = (q + 1) % 2 if layer else q % 2
                    x_n = None
                    if layer == 0 and (g == 0 or groups[g - 1][0] == 1):
                        x_n = 16 * N_X if q < 0 else bt * (32 * N_X) + 16 * N_X * (2 + q // 2)
                    product(groups_before(t, g), prod_slot(q, g), j % 2, par, a, x_n,
                            rhs_before(t, j) + 1 if first_of(groups, g) else None)

            each_chunk(dve, chunk)
            dve.wait_ge(h2_copied, CHUNKS)
            sum_over_d(1, h2, CHUNKS - 1)

        @block.scalar
        def _(act):
            def copy_rhs(n, slot, bank, loads, free):
                act.wait_ge(rhs_loaded[slot], loads)
                if free is not None:
                    act.wait_ge(prod_ready, free)
                act.activation(rhs[:, bank, :], rhs_ring[:, slot, :], ACT.Copy).then_inc(rhs_ready, 1)

            def copy_xt(k, before):
                act.wait_ge(turned, before + 1)
                dst = xt[:, :, 4 * k:4 * k + 4].rearrange("f b d -> f d b")
                act.activation(dst, turn[0:FIELDS, :].rearrange("f (d b) -> f d b", d=4), ACT.Copy).then_inc(turn_copied, 1)

            def store_xt(bt, before):
                act.wait_ge(turn_copied, before)
                act.dma_start(x_dram[:, bass.ds(bt * (P * DIM), P * DIM)], xt[:].rearrange("f b d -> f (b d)")).then_inc(x_stored, 16)

            def copy_h1(t):
                act.wait_ge(prod_used, t * N_G + len(L0) - (N_G - L0_END if not isinstance(t, int) or t > 0 else 0))
                if not isinstance(t, int) or t > 0:
                    act.wait_ge(h1_stored, t * 16)
                    act.wait_ge(z_summed, 1 if isinstance(t, int) and t == 1 else t * 2 - 2)
                act.activation(h1[:], acc0[:], ACT.Copy).then_inc(h1_copied, 1)
                act.wait_ge(h1_copied, t + 1)
                act.dma_start(h1_dram[:, bass.ds(t * CH, CH)], h1[:]).then_inc(h1_stored, 16)

            def copy_h2(t, par):
                act.wait_ge(prod_used, groups_before(t + 1, 0) - (len(L0) if is_last(t) else 0))
                act.activation(h2[:], acc1[:, par, :], ACT.Copy).then_inc(h2_copied, 1)

            def copy_h2t(before):
                act.wait_ge(turned, before + 1)
                act.activation(h2t[:].rearrange("p s n -> p (s n)"), turn[:], ACT.Copy).then_inc(turn_copied, 1)

            def copy_g(bt, q, s):
                act.wait_ge(g_done, bt * (PER_BLOCK * SUB) + (q * SUB + s + 1))
                b0 = q * SAMPLES + s * SUB_B
                act.activation(gsum[:, :, b0:b0 + SUB_B].rearrange("p i b -> p b i"),
                               gbank[:, s % 2, :].rearrange("p (b i) -> p b i", i=FIELDS),
                               ACT.Copy).then_inc(g_free, 1)

            def copy_z3(bt):
                act.wait_ge(w2_free, bt * F_LOADS + (W2_SLOTS + F_LOADS))
                act.activation(z[:, 2, bass.ds(bt * P, P)], gbank[:, 0, 0:P], ACT.Copy).then_inc(g_free, 2)

            act.sem_inc(g_free, 2)
            for k in range(4):
                copy_xt(k, k)
            store_xt(0, 4)
            for c in range(N_Y):
                copy_rhs(c, c, c % 2, 16, None if c < 2 else sum(1 for x in L0 if x[3] <= c - 2))

            def chunk(bt, q, t):
                last = is_last(t)
                groups = GROUPS_LAST if last else GROUPS
                before = turns_before(bt, q)

                def copy(j):
                    n_before = sum(1 for x in groups if x[3] <= j - 2)
                    if j < 2:
                        n_before = 0
                        if j == 0:
                            n_before = -(N_X // PAIR)
                    slot = (N_Y + j) % RING
                    loads = t * (16 * N_R // RING) + 16 * ((N_Y + j) // RING + 1)
                    copy_rhs(None, slot, j % 2, loads, groups_before(t, n_before))

                for g, (layer, c, a, j) in enumerate(groups):
                    if first_of(groups, g):
                        if j == 0:
                            if q < 0:
                                copy_h1(0)
                            copy(0)
                            if q >= 0:
                                copy_h2(t - 1, q % 2)
                        if j + 1 <= groups[-1][3]:
                            copy(j + 1)
                    if g == XCOL_AT:
                        act.wait_ge(turned, before + 1)
                        act.activation(xcol[:, (q + 1) % 2], turn[:, 0:SUB * FIELDS].rearrange("p (s f) -> p s f", s=SUB),
                                       ACT.Copy).then_inc(turn_copied, 1)
                        before = before + 1
                    if g in XT_AT and makes_xt(bt, q):
                        if g == XT_AT[0]:
                            act.wait_ge(x_stored, bt * 16 + 16)
                        copy_xt(XT_AT.index(g), before)
                        before = before + 1
                        if g == XT_AT[-1]:
                            store_xt(bt + 1, before)
                    if q >= 0 and g == H2T_AT:
                        copy_h2t(before)
                    if q >= 0 and g in G_AT:
                        copy_g(bt, q, G_AT.index(g))
                    if g == L0_END and not last:
                        copy_h1(t + 1)
                if q == 3:
                    copy_z3(bt)

            each_chunk(act, chunk)
            copy_h2(CHUNKS - 1, (CHUNKS - 1) % 2)
            copy_h2t(turns_before(BLOCKS - 1, 2) + 2)
            for s in range(SUB):
                copy_g(BLOCKS - 1, PER_BLOCK - 1, s)
            copy_z3(BLOCKS - 1)
            act.wait_ge(top_loaded, 16 * 7)
            for m in range(4):
                act.wait_ge(hid_done, m + 1)
                act.activation(hid1[:, m, :], rhs[:, m % 2, :], ACT.Relu, bias=bt1[:, m:m + 1]).then_inc(hid_copied, 1)
            for m in range(2):
                act.wait_ge(hid_done, 5 + m)
                act.activation(hid2[:, m, :], acc1[:, m, :], ACT.Relu, bias=bt2[:, m:m + 1]).then_inc(hid_copied, 1)
            act.wait_ge(hid_done, 7)
            act.activation(y, acc0[0:1, :], ACT.Copy).then_inc(hid_copied, 1)

        @block.tensor
        def _(pe):
            def turn_xt(k, bt, before):
                if k == 0:
                    pe.wait_ge(rows_gathered, bt * (16 * FIELDS) + 16 * FIELDS)
                    pe.sem_inc(pe_passed, 1)
                if not isinstance(before, int) or before > 0:
                    pe.wait_ge(turn_copied, before)
                    pe.sem_inc(pe_passed, 1)
                for d in range(4):
                    last = pe.transpose(turn[0:FIELDS, d * P:(d + 1) * P], rows[:, :, 4 * k + d], ident[:])
                last.then_inc(turned, 1)

            def contract(acc, n, slot, weights, first, last):
                pe.wait_ge(prod_ready, n + 1)
                for k, w in enumerate(weights):
                    mm = pe.matmul(acc, w, prod[:, slot, k, :], start=first and k == 0,
                                   stop=last and k == PAIR - 1, skip_group_check=True)
                mm.then_inc(prod_used, 1)

            def layer0(g, n, slot):
                _, c, a, _ = L0[g]
                k = W0_TILES.index((c, a))
                contract(acc0[:], n, slot, [w0[:, k + i, :] for i in range(PAIR)],
                         g == 0, g == len(L0) - 1)

            def turn_h2(before):
                pe.wait_ge(turn_copied, before)
                for s in range(SUB):
                    last = pe.transpose(turn[:, s * P:(s + 1) * P], h2[:, s * P:(s + 1) * P], ident[:])
                last.then_inc(turned, 1)

            def form_g(bt, q, s, h2t_copied):
                if s == 0:
                    pe.wait_ge(turn_copied, h2t_copied)
                pe.wait_ge(xdiag_ready, bt * (PER_BLOCK * SUB) + (q * SUB + s + 1))
                pe.wait_ge(g_free, g_before(bt, q, s) + 1)
                pe.matmul(gbank[:, s % 2, :], h2t[:, s, :], xdiag[:, s % 2].rearrange("p b i -> p (b i)"),
                          start=True, stop=True).then_inc(g_done, 1)

            def contract_w2(bt, k):
                if k == 0:
                    pe.wait_ge(g_free, bt * 18 + 18)
                pe.wait_ge(w2_loaded[k % W2_SLOTS], bt * (16 * F_LOADS // W2_SLOTS) + 16 * (k // W2_SLOTS + 1))
                for i in range(W2_I):
                    mm = pe.matmul(gbank[:, 0, 0:P], w2[:, k % W2_SLOTS, i, :], gsum[:, k * W2_I + i, :],
                                   start=k == 0 and i == 0, stop=k == F_LOADS - 1 and i == W2_I - 1,
                                   skip_group_check=True)
                mm.then_inc(w2_free, 1)

            pe.sem_inc(w2_free, W2_SLOTS)
            pe.wait_ge(consts_loaded, 32)
            for k in range(4):
                turn_xt(k, 0, k)
            pe.wait_ge(w0_summed, 1)
            for g in range(len(L0)):
                layer0(g, g, g % PROD)

            def chunk(bt, q, t):
                last = is_last(t)
                groups = GROUPS_LAST if last else GROUPS
                before = turns_before(bt, q)
                for g, (layer, c, a, j) in enumerate(groups):
                    if g == XCOL_AT:
                        pe.wait_ge(turn_copied, before)
                        pe.sem_inc(pe_passed, 1)
                        for s in range(SUB):
                            xs = xt[:, (q + 1) % 4 * SAMPLES + s * SUB_B:(q + 1) % 4 * SAMPLES + (s + 1) * SUB_B, :]
                            mm = pe.transpose(turn[:, s * FIELDS:(s + 1) * FIELDS], xs.rearrange("f b d -> f (b d)"),
                                              ident[0:FIELDS, 0:FIELDS])
                        mm.then_inc(turned, 1)
                        before = before + 1
                    if g in XT_AT and makes_xt(bt, q):
                        turn_xt(XT_AT.index(g), bt + 1, before)
                        before = before + 1
                    if q >= 0 and g == H2T_AT:
                        pe.wait_ge(h2_copied, t)
                        turn_h2(before)
                        before = before + 1
                    if q >= 0 and g in G_AT:
                        form_g(bt, q, G_AT.index(g), before)
                    if q == 3 and F_AT <= g < F_AT + F_LOADS:
                        contract_w2(bt, g - F_AT)
                    n, slot = groups_before(t, g), prod_slot(q, g)
                    if layer == 0:
                        if g == len(L1_A):
                            pe.wait_ge(h1_copied, t + 1)
                        layer0(g - len(L1_A), n, slot)
                    else:
                        if q < 0 and a == 0:
                            pe.wait_ge(w1_loaded[c], 16)
                        contract(acc1[:, (q + 1) % 2, :], n, slot, [w1[:, c, a + i, :] for i in range(PAIR)],
                                 g == 0, g == len(groups) - 1)

            each_chunk(pe, chunk)
            pe.wait_ge(h2_copied, CHUNKS)
            tail = turns_before(BLOCKS - 1, 2) + 2
            turn_h2(tail)
            for s in range(SUB):
                form_g(BLOCKS - 1, PER_BLOCK - 1, s, tail + 1)
            for k in range(F_LOADS):
                contract_w2(BLOCKS - 1, k)

            pe.wait_ge(top_loaded, 16 * 7)
            pe.wait_ge(z_summed, 2 * CHUNKS)
            pe.wait_ge(g_free, BLOCKS * 18 + 2)
            for m in range(4):
                if m >= 2:
                    pe.wait_ge(hid_copied, m - 1)
                for k in range(3):
                    pe.matmul(rhs[:, m % 2, :], wt1[:, k, m * P:(m + 1) * P], z[:, k, :], start=k == 0, stop=False)
                pe.matmul(rhs[:, m % 2, :], wt1[0:DENSE, 3, m * P:(m + 1) * P], dense,
                          start=False, stop=True).then_inc(hid_done, 1)
            for m in range(2):
                for k in range(4):
                    pe.wait_ge(hid_copied, k + 1)
                    mm = pe.matmul(acc1[:, m, :], wt2[:, k, m * P:(m + 1) * P], hid1[:, k, :], start=k == 0, stop=k == 3)
                mm.then_inc(hid_done, 1)
            for k in range(2):
                pe.wait_ge(hid_copied, 5 + k)
                mm = pe.matmul(acc0[0:1, :], wt3[:, k:k + 1], hid2[:, k, :], start=k == 0, stop=k == 1)
            mm.then_inc(hid_done, 1)


def kernel(**inputs):
    import numpy as np
    import concourse.bacc as bacc
    from concourse.bass_utils import run_bass_kernel_spmd

    f = {k: np.ascontiguousarray(np.asarray(v)) for k, v in inputs.items()}
    arrays = {f"tbl_{i}": f[f"tbl_{i}"] for i in range(FIELDS)}
    arrays["ids"] = f["ids"]
    for name in ("W_top1", "W_top2"):
        arrays[name] = f[name]
    pairs0 = f["L0_rec_W0"].reshape(FIELDS, FIELDS, NF)
    there, back = [], []
    for c, a in W0_TILES:
        i, j = slice(a * XA, (a + 1) * XA), slice(c * RB, (c + 1) * RB)
        there.append(pairs0[i, j].reshape(P, NF))
        other = pairs0[j, i].transpose(1, 0, 2).reshape(P, NF)
        back.append(other if a < 2 * c else np.zeros_like(other))
    arrays["w0_tiles"] = np.ascontiguousarray(np.stack([np.stack(there, 1), np.stack(back, 1)]))
    pairs1 = f["L0_rec_W1"].reshape(N_X, XA, N_H, RB, NF)
    arrays["w1_tiles"] = np.ascontiguousarray(pairs1.transpose(1, 3, 2, 0, 4).reshape(P, N_H, N_X, NF))
    arrays["w2_rows"] = np.ascontiguousarray(f["L0_rec_W2"].reshape(FIELDS, NF, NF).transpose(1, 0, 2))
    arrays["w_top3_cols"] = np.ascontiguousarray(f["W_top3"].reshape(2, P).T)
    arrays["b_top1_cols"] = np.ascontiguousarray(f["b_top1"].reshape(4, P).T)
    arrays["b_top2_cols"] = np.ascontiguousarray(f["b_top2"].reshape(2, P).T)
    arrays["dense_rows"] = np.ascontiguousarray(f["dense_ctx"].T)
    arrays["identity"] = np.eye(P, dtype=np.float32)
    arrays["sample_mask"] = np.ascontiguousarray(np.kron(np.eye(SUB_B), np.ones((DIM, 1))).astype(np.float32))

    nc = bacc.Bacc("TRN2", target_bir_lowering=False, num_devices=1)
    ins = {k: nc.dram_tensor(k, a.shape, mybir.dt.from_np(a.dtype), kind="ExternalInput").ap() for k, a in arrays.items()}
    out = nc.dram_tensor("out", (BATCH, 1), F32, kind="ExternalOutput").ap()
    build(nc, ins, out)
    r = run_bass_kernel_spmd(nc, [arrays], core_ids=[0])
    return r.results[0]["out"]
```

```python
from contextlib import ExitStack

import concourse.bass as bass
from concourse import mybir

F32 = mybir.dt.float32
F32R = mybir.dt.float32r
I32 = mybir.dt.int32
U32 = mybir.dt.uint32
ALU = mybir.AluOpType
ACT = mybir.ActivationFunctionType
AX_X = mybir.AxisListType.X

P = 128
FIELDS, DIM, BATCH = 64, 16, 512
NF = 128
CH = 512
SAMPLES = CH // DIM
CHUNKS = BATCH * DIM // CH
PER_BLOCK = P // SAMPLES
BLOCKS = CHUNKS // PER_BLOCK
XA, RB = 8, 16
N_X = FIELDS // XA
N_Y = FIELDS // RB
N_H = NF // RB
PAIR = 2
SUB = CH // P
SUB_B = P // DIM
HALF_B = SUB_B // 2
RING = 4
PROD = 6
HI = 3
LAG = 2
W2_I, W2_SLOTS = 4, 2
HIDDEN1, HIDDEN2, DENSE = 512, 256, 16

LAYER1_EARLY = 6
L1_A = [(1, c, a, c) for c in range(LAYER1_EARLY) for a in range(0, N_X, PAIR)]
L0 = [(0, c, a, c) for c in range(N_Y) for a in range(0, 2 * c + 2, PAIR)]
L0_MID = [(l, c, a, j + LAYER1_EARLY) for l, c, a, j in L0]
L1_B = [(1, c, a, c + N_Y) for c in range(LAYER1_EARLY, N_H) for a in range(0, N_X, PAIR)]
GROUPS = L1_A + L0_MID + L1_B
GROUPS_LAST = L1_A + [(1, c, a, c) for c in range(LAYER1_EARLY, N_H) for a in range(0, N_X, PAIR)]
N_G, N_R = len(GROUPS), N_Y + N_H
L0_END = len(L1_A) + len(L0)
W0_TILES = [(c, a) for c in range(N_Y) for a in range(2 * c + 2)]

KINDS = ("pool", "dve", "pool", "raw")


def kind_of(group):
    layer, _, a, _ = group
    return KINDS[a // PAIR] if layer else "raw"


def places(groups, *kinds):
    return [g for g, x in enumerate(groups) if kind_of(x) in kinds]


def split_places(groups):
    return places(groups, "pool", "dve")


N_SPLIT, N_POOL, N_DVE = (len(places(GROUPS, *k)) for k in (("pool", "dve"), ("pool",), ("dve",)))
W1_SPLIT = {(c, a + i): n for n, (c, a, i) in enumerate(
    (c, a, i) for c in range(N_H) for a in range(0, N_X, PAIR) if KINDS[a // PAIR] != "raw" for i in range(PAIR))}
W1_RAW = {(c, a + i): n for n, (c, a, i) in enumerate(
    (c, a, i) for c in range(N_H) for a in range(0, N_X, PAIR) if KINDS[a // PAIR] == "raw" for i in range(PAIR))}

XCOL_AT = 0
XT_AT = (1, 2, 3, 4)
H2T_AT = 6
G_AT = (9, 13)
F_LOADS = FIELDS // W2_I
F_AT = tuple(16 + 3 * k // 2 for k in range(F_LOADS))


X_LOADS_AT = 5
RHS_LEAD = 8
NEXT_H_AT = L0_END + 4


def first_of(groups, g):
    return g == 0 or groups[g - 1][3] != groups[g][3]


def first_place(groups, j):
    return next(g for g, x in enumerate(groups) if x[3] == j)


def groups_before(t, g):
    return t * N_G + (len(L0) + g)


def rhs_before(t, j):
    return t * N_R + (N_Y + j)


def prod_slot(q, g):
    return (len(L0) + N_G * (q + 1) + g) % PROD


assert PER_BLOCK * N_G % PROD == 0


def back(groups, start, g, depth, *kinds):
    here = places(groups, *kinds)
    ahead = L0 if start else GROUPS
    there = [x - len(ahead) for x in places(ahead, *kinds)]
    every = there + here
    at = every.index(g) - depth
    return every[at] if at >= 0 else None


def side_before(bt, q):
    if q < 0:
        return 4
    return bt * 21 + (5 + 4 * q + (4 if q > 2 else 0))


def build(nc, ins, out):
    with ExitStack() as ctx:
        def sb(name, shape, dt=F32):
            return ctx.enter_context(nc.sbuf_tensor(f"{name}_sb", shape, dt))

        def psum(name, shape):
            return ctx.enter_context(nc.psum_tensor(name, shape, F32))

        def sem(name):
            return ctx.enter_context(nc.semaphore(name))

        x_dram = nc.dram_tensor("x_scratch", [FIELDS, CHUNKS * CH], F32, kind="Internal").ap()
        h1_dram = nc.dram_tensor("h1_scratch", [NF, CHUNKS * CH], F32, kind="Internal").ap()

        ident = sb("ident", [P, P])
        mask = sb("mask", [P, HALF_B])
        w0 = sb("w0", [P, len(W0_TILES), NF])
        w1_raw = sb("w1_raw", [P, len(W1_RAW), NF])
        w1_hi = sb("w1_hi", [P, len(W1_SPLIT), NF], F32R)
        w1_lo = sb("w1_lo", [P, len(W1_SPLIT), NF], F32R)
        w2 = sb("w2", [P, W2_SLOTS, W2_I, NF])
        ids = sb("ids", [P, BLOCKS, FIELDS], I32)
        ids_now = sb("ids_now", [P, FIELDS], I32)
        rows = sb("rows", [P, FIELDS, DIM])
        xt = sb("xt", [FIELDS, P, DIM])
        x_tiles = sb("x_tiles", [P, 2, N_X, CH])
        rhs_ring = sb("rhs_ring", [P, RING, CH])
        hi = sb("hi", [P, HI, PAIR, CH], F32R)
        ring_at = -(-nc.sbuf_base // 32) * 32
        sb("prod_space", [P, PROD, PAIR, CH])
        prod = nc.alloc_sbuf_tensor_at("prod_sb", [P, PROD, PAIR, CH], F32, offset=ring_at)
        lo = nc.alloc_sbuf_tensor_at("lo_sb", [P, PROD, PAIR, CH], F32R, offset=ring_at)
        h1 = sb("h1", [NF, CH])
        h2 = sb("h2", [NF, CH])
        h2t = sb("h2t", [P, SUB, NF])
        xcol = sb("xcol", [P, 2, SUB, FIELDS])
        xdiag = sb("xdiag", [P, 2, HALF_B, FIELDS])
        gsum = sb("gsum", [NF, FIELDS, P])
        z = sb("z", [NF, 3, BATCH])
        w0_back = x_tiles[:, 1].rearrange("p a n -> p (a n)")[:, 0:len(W0_TILES) * NF]
        w1_whole = gsum[:].rearrange("p i b -> p (i b)")[:, 0:len(W1_SPLIT) * NF]
        w1_hi_flat = w1_hi[:].rearrange("p k n -> p (k n)")
        w1_lo_flat = w1_lo[:].rearrange("p k n -> p (k n)")
        top = x_tiles[:, 0].rearrange("p a n -> p (a n)")
        wt1 = top[:, 0:4 * HIDDEN1].rearrange("p (k n) -> p k n", k=4)
        wt2 = top[:, 2048:2048 + 4 * HIDDEN2].rearrange("p (k n) -> p k n", k=4)
        wt3 = top[:, 3072:3072 + 2]
        bt1 = top[:, 3080:3084]
        bt2 = top[:, 3088:3090]
        dense = top[0:DENSE, 3584:3584 + BATCH]
        hid1 = x_tiles[:, 1, 0:4, :]
        hid2 = x_tiles[:, 1, 4:6, :]
        y = x_tiles[0:1, 1, 6, :]

        acc = psum("acc", [P, 2, CH])
        rhs = psum("rhs", [P, 2, CH])
        prod_ps = psum("prod_ps", [P, PAIR, CH])
        side = psum("side", [P, 2, CH])

        ids_loaded = sem("ids_loaded")
        consts_loaded = sem("consts_loaded")
        w0_loaded = sem("w0_loaded")
        w0_summed = sem("w0_summed")
        w1_loaded = sem("w1_loaded")
        w1_hi_ready = sem("w1_hi_ready")
        w1_lo_ready = sem("w1_lo_ready")
        w2_loaded = [sem(f"w2_loaded{k}") for k in range(W2_SLOTS)]
        w2_free = sem("w2_free")
        top_loaded = sem("top_loaded")
        ids_copied = sem("ids_copied")
        rows_gathered = sem("rows_gathered")
        x_stored = sem("x_stored")
        x_loaded = [sem(f"x_loaded{k}") for k in range(2)]
        rhs_loaded = [sem(f"rhs_loaded{k}") for k in range(RING)]
        rhs_ready = sem("rhs_ready")
        prod_ready = sem("prod_ready")
        hi_ready = sem("hi_ready")
        lo_pool_ready = sem("lo_pool_ready")
        lo_dve_ready = sem("lo_dve_ready")
        prod_used = sem("prod_used")
        h1_copied = sem("h1_copied")
        h1_stored = sem("h1_stored")
        h2_copied = sem("h2_copied")
        side_filled = sem("side_filled")
        side_copied = sem("side_copied")
        xdiag_ready = sem("xdiag_ready")
        z_summed = sem("z_summed")
        hid_done = sem("hid_done")
        hid_copied = sem("hid_copied")
        y_stored = sem("y_stored")
        pe_passed = sem("pe_passed")
        pool_passed = sem("pool_passed")

        block = ctx.enter_context(nc.Block())

        def each_chunk(eng, chunk):
            chunk(0, -1, 0)
            with eng.Fori(0, BLOCKS - 1) as bt:
                for q in range(PER_BLOCK):
                    chunk(bt, q, bt * PER_BLOCK + (q + 1))
            for q in range(PER_BLOCK - 1):
                chunk(BLOCKS - 1, q, (BLOCKS - 1) * PER_BLOCK + q + 1)

        def is_last(t):
            return isinstance(t, int) and t == CHUNKS - 1

        def groups_of(t):
            return GROUPS_LAST if is_last(t) else GROUPS

        def makes_xt(bt, q):
            return q == 2 and not (isinstance(bt, int) and bt == BLOCKS - 1)

        def wait_lo(eng, kind, t, index):
            if kind == "pool":
                eng.wait_ge(lo_pool_ready, t * N_POOL + (index + 1))
            else:
                eng.wait_ge(lo_dve_ready, t * N_DVE + (index + 1))

        @block.sync
        def _(sp):
            def load_x(t, par):
                cols = bass.ds(t * CH, CH)
                for a in range(N_X):
                    src = x_dram[a * XA:(a + 1) * XA, cols].unsqueeze(1).to_broadcast([XA, RB, CH])
                    sp.dma_start(x_tiles[:, par, a, :], src).then_inc(x_loaded[par], 16)

            def load_rhs(slot, src):
                rep = src.unsqueeze(0).to_broadcast([XA, RB, CH])
                sp.dma_start(rhs_ring[:, slot, :], rep).then_inc(rhs_loaded[slot], 16)

            sp.dma_start(ids[:], ins["ids"].rearrange("(t p) f -> p t f", p=P)).then_inc(ids_loaded, 16)
            sp.dma_start(ident[:], ins["identity"]).then_inc(consts_loaded, 16)
            sp.dma_start(mask[:], ins["sample_mask"]).then_inc(consts_loaded, 16)
            sp.dma_start(w0[:], ins["w0_tiles"][0]).then_inc(w0_loaded, 16)
            sp.dma_start(w0_back, ins["w0_tiles"][1].rearrange("p t n -> p (t n)")).then_inc(w0_loaded, 16)
            sp.dma_start(w1_whole, ins["w1_split"]).then_inc(w1_loaded, 16)
            sp.dma_start(w1_raw[:], ins["w1_raw"]).then_inc(w1_loaded, 16)

            sp.wait_ge(x_stored, 16)
            load_x(0, 0)
            for c in range(N_Y):
                load_rhs(c % RING, x_dram[c * RB:(c + 1) * RB, 0:CH])

            def w2_load(bt, k):
                sp.wait_ge(w2_free, bt * F_LOADS + (k + 1))
                sp.dma_start(w2[:, k % W2_SLOTS], ins["w2_rows"][:, k * W2_I:(k + 1) * W2_I, :]).then_inc(
                    w2_loaded[k % W2_SLOTS], 16)

            def load_place(q, t, j, last=False):
                if not (q < 0 and N_Y + j < RING):
                    sp.wait_ge(rhs_ready, rhs_before(t, j - (RING - 1)))
                layer, c = next((x[0], x[1]) for x in (GROUPS_LAST if last else GROUPS) if x[3] == j)
                source, cols = (h1_dram, bass.ds(t * CH, CH)) if layer else (x_dram, bass.ds(t * CH + CH, CH))
                load_rhs((N_Y + j) % RING, source[c * RB:(c + 1) * RB, cols])

            def first_places(t, q):
                sp.wait_ge(h1_stored, t * 16 + 16)
                for j in range(2):
                    load_place(q, t, j)

            first_places(0, -1)

            def chunk(bt, q, t):
                last = is_last(t)
                w2_done = 0
                for g in range(len(groups_of(t))):
                    if g == X_LOADS_AT:
                        sp.wait_ge(prod_ready, groups_before(t, 0))
                        if q < 0:
                            sp.wait_ge(w0_summed, 1)
                        if q == 2 and not last:
                            sp.wait_ge(x_stored, bt * 16 + 32)
                        if not last:
                            load_x(t + 1, q % 2)
                        else:
                            for dst, src in (
                                (wt1[:, 0:3, :], ins["W_top1"][0:3 * P, :].rearrange("(k p) n -> p k n", p=P)),
                                (wt1[0:DENSE, 3, :], ins["W_top1"][3 * P:3 * P + DENSE, :]),
                                (wt2, ins["W_top2"].rearrange("(k p) n -> p k n", p=P)),
                                (wt3, ins["w_top3_cols"]), (bt1, ins["b_top1_cols"]),
                                (bt2, ins["b_top2_cols"]), (dense, ins["dense_rows"]),
                            ):
                                sp.dma_start(dst, src).then_inc(top_loaded, 16)
                    for j in range(2, N_H if last else N_R):
                        if g == max(first_place(groups_of(t), j) - RHS_LEAD, 0):
                            load_place(q, t, j, last)
                    while q == 3 and w2_done < F_LOADS and F_AT[max(w2_done - W2_SLOTS, 0)] < g:
                        w2_load(bt, w2_done)
                        w2_done += 1
                    if g == NEXT_H_AT and not last:
                        first_places(t + 1, (q + 1) % PER_BLOCK)
                for k in range(w2_done, F_LOADS if q == 3 else 0):
                    w2_load(bt, k)

            each_chunk(sp, chunk)
            for k in range(F_LOADS):
                w2_load(BLOCKS - 1, k)
            sp.wait_ge(hid_copied, 7)
            sp.dma_start(out.rearrange("b o -> o b"), y).then_inc(y_stored, 16)
            sp.wait_ge(y_stored, 16)

        @block.gpsimd
        def _(pool):
            def gather(bt, part):
                if part == 0:
                    if not isinstance(bt, int) or bt > 0:
                        pool.wait_ge(rows_gathered, bt * (16 * FIELDS))
                    pool.tensor_copy(ids_now[:], ids[:, bass.ds(bt, 1), :].rearrange("p o f -> p (o f)")).then_inc(ids_copied, 1)
                    pool.wait_ge(ids_copied, bt + 1)
                    pool.sem_inc(pool_passed, 1)
                for f in range(part * FIELDS // 4, (part + 1) * FIELDS // 4):
                    pool.indirect_dma_start(
                        rows[:, f, :], None, ins[f"tbl_{f}"],
                        bass.IndirectOffsetOnAxis(ap=ids_now[:, f:f + 1].bitcast(U32), axis=0),
                    ).then_inc(rows_gathered, 16)

            def diagonal(bt, q, half):
                for s in range(2 * half, 2 * half + 2):
                    src = xcol[:, q % 2, s, :].unsqueeze(1).to_broadcast([P, HALF_B, FIELDS])
                    on = mask[:].unsqueeze(2).to_broadcast([P, HALF_B, FIELDS])
                    pool.tensor_tensor(xdiag[:, s % 2], src, on, ALU.mult).then_inc(xdiag_ready, 1)

            def chunk(bt, q, t, to_gather=None):
                groups = groups_of(t)
                before = side_before(bt, q)
                g_uses = before + (6 if makes_xt(bt, q) else 2)
                for g, x in enumerate(groups):
                    if g == 0 and q >= 0:
                        pool.wait_ge(side_copied, before)
                        diagonal(bt, q, 0)
                    if g == G_AT[0] + 1 and q >= 0:
                        pool.wait_ge(side_filled, g_uses + 1)
                        diagonal(bt, q, 1)
                    if g == len(L1_A) and to_gather:
                        if to_gather[1] == 0:
                            pool.wait_ge(side_copied, before + 5)
                        gather(*to_gather)
                    if kind_of(x) == "pool":
                        subtract(groups, q, t, g)

            def subtract(groups, q, t, g):
                e, slot = split_places(groups).index(g), prod_slot(q, g)
                pool.wait_ge(hi_ready, t * N_SPLIT + (e + 1))
                pool.tensor_tensor(lo[:, slot], prod[:, slot], hi[:, e % HI].bitcast(F32),
                                   ALU.subtract).then_inc(lo_pool_ready, 1)

            pool.wait_ge(ids_loaded, 16)
            for part in range(4):
                gather(0, part)
            pool.wait_ge(consts_loaded, 32)
            pool.wait_ge(side_copied, 4)
            gather(1, 0)
            chunk(0, -1, 0, (1, 1))
            chunk(0, 0, 1, (1, 2))
            chunk(0, 1, 2, (1, 3))
            with pool.Fori(0, BLOCKS - 2) as bt:
                for part in range(4):
                    here = (bt, part + 2) if part < 2 else (bt + 1, part - 2)
                    chunk(*here, bt * PER_BLOCK + (3 + part), (bt + 2, part))
            for t in range(PER_BLOCK * (BLOCKS - 2) + 3, CHUNKS):
                chunk((t - 1) // PER_BLOCK, (t - 1) % PER_BLOCK, t)
            pool.wait_ge(side_copied, side_before(BLOCKS - 1, 2) + 4)
            diagonal(BLOCKS - 1, 3, 0)
            pool.wait_ge(side_filled, side_before(BLOCKS - 1, 2) + 4 + 2)
            diagonal(BLOCKS - 1, 3, 1)

        @block.vector
        def _(dve):
            dve.wait_ge(w0_loaded, 32)
            w0_flat = w0[:].rearrange("p t n -> p (t n)")
            dve.tensor_tensor(w0_flat, w0_flat, w0_back, ALU.add).then_inc(w0_summed, 1)
            dve.wait_ge(w1_hi_ready, 1)
            dve.tensor_tensor(w1_lo_flat, w1_whole, w1_hi_flat.bitcast(F32), ALU.subtract).then_inc(w1_lo_ready, 1)

            def operands(par, a, bank):
                return x_tiles[:, par, a:a + PAIR, :], rhs[:, bank:bank + 1, :].to_broadcast([P, PAIR, CH])

            def sum_over_d(layer, src, t):
                dve.tensor_reduce(
                    z[:, layer, bass.ds(t * SAMPLES, SAMPLES)], src[:].rearrange("p (b d) -> p b d", d=DIM),
                    AX_X, ALU.add).then_inc(z_summed, 1)

            for g, (_, c, a, j) in enumerate(L0):
                if first_of(L0, g):
                    dve.wait_ge(rhs_ready, j + 1)
                if g == 0:
                    dve.wait_ge(x_loaded[0], 16 * N_X)
                if g >= PROD:
                    dve.wait_ge(prod_used, g - (PROD - 1))
                dve.tensor_tensor(prod[:, g % PROD], *operands(0, a, j % 2), ALU.mult).then_inc(prod_ready, 1)
            dve.wait_ge(h1_copied, 1)
            sum_over_d(0, h1, 0)

            def product(groups, bt, q, t, g):
                layer, c, a, j = groups[g]
                kind = kind_of(groups[g])
                if first_of(groups, g):
                    dve.wait_ge(rhs_ready, rhs_before(t, j) + 1)
                if layer == 0 and g == len(L1_A):
                    dve.wait_ge(x_loaded[q % 2], 16 * N_X if q < 0 else bt * (32 * N_X) + 16 * N_X * (2 + q // 2))
                par = (q + 1) % 2 if layer else q % 2
                if kind == "dve":
                    d = places(groups, "dve").index(g)
                    if q >= 0 or d > 0:
                        dve.wait_ge(lo_dve_ready, t * N_DVE + d)
                    dve.tensor_tensor(prod_ps[:], *operands(par, a, j % 2), ALU.mult).then_inc(prod_ready, 1)
                    return
                wait_slot(t, g)
                dve.tensor_tensor(prod[:, prod_slot(q, g)], *operands(par, a, j % 2), ALU.mult).then_inc(prod_ready, 1)

            def wait_slot(t, g):
                dve.wait_ge(prod_used, groups_before(t, g - (PROD - 1)))

            def subtract(groups, q, t, g):
                e = split_places(groups).index(g)
                dve.wait_ge(hi_ready, t * N_SPLIT + (e + 1))
                wait_slot(t, g)
                dve.tensor_tensor(lo[:, prod_slot(q, g)], prod_ps[:], hi[:, e % HI].bitcast(F32),
                                  ALU.subtract).then_inc(lo_dve_ready, 1)

            def chunk(bt, q, t):
                last = is_last(t)
                groups = groups_of(t)
                for g in range(len(groups)):
                    if g == 8 and q >= 0:
                        dve.wait_ge(h2_copied, t)
                        sum_over_d(1, h2, t - 1)
                    if g == L0_END + 3 and not last:
                        dve.wait_ge(h1_copied, t + 2)
                        sum_over_d(0, h1, t + 1)
                    product(groups, bt, q, t, g)
                    if g > 0 and kind_of(groups[g - 1]) == "dve":
                        subtract(groups, q, t, g - 1)

            each_chunk(dve, chunk)
            dve.wait_ge(h2_copied, CHUNKS)
            sum_over_d(1, h2, CHUNKS - 1)

        @block.scalar
        def _(act):
            def copy_rhs(slot, bank, loads, free):
                act.wait_ge(rhs_loaded[slot], loads)
                if free is not None:
                    act.wait_ge(prod_ready, free)
                act.activation(rhs[:, bank, :], rhs_ring[:, slot, :], ACT.Copy).then_inc(rhs_ready, 1)

            def copy_xt(k, before):
                act.wait_ge(side_filled, before + 1)
                dst = xt[:, :, 4 * k:4 * k + 4].rearrange("f b d -> f d b")
                act.activation(dst, side[0:FIELDS, 0, :].rearrange("f (d b) -> f d b", d=4), ACT.Copy).then_inc(side_copied, 1)

            def store_xt(bt, before):
                act.wait_ge(side_copied, before)
                act.dma_start(x_dram[:, bass.ds(bt * (P * DIM), P * DIM)], xt[:].rearrange("f b d -> f (b d)")).then_inc(x_stored, 16)

            def copy_h1(t, bank):
                first = isinstance(t, int) and t == 0
                act.wait_ge(prod_used, len(L0) if first else groups_before(t, L0_END - N_G))
                if not first:
                    act.wait_ge(h1_stored, t * 16)
                    act.wait_ge(z_summed, 1 if isinstance(t, int) and t == 1 else t * 2 - 2)
                act.activation(h1[:], acc[:, bank, :], ACT.Copy).then_inc(h1_copied, 1)
                act.wait_ge(h1_copied, t + 1)
                act.dma_start(h1_dram[:, bass.ds(t * CH, CH)], h1[:]).then_inc(h1_stored, 16)

            def copy_h2(t, bank):
                act.wait_ge(prod_used, groups_before(t + 1, 0) - (len(L0) if is_last(t) else 0))
                act.activation(h2[:], acc[:, bank, :], ACT.Copy).then_inc(h2_copied, 1)

            def copy_h2t(before):
                act.wait_ge(side_filled, before + 1)
                act.activation(h2t[:].rearrange("p s n -> p (s n)"), side[:, 0, :], ACT.Copy).then_inc(side_copied, 1)

            def copy_g(q, use, before):
                act.wait_ge(side_filled, before + 1)
                for m in range(2):
                    for s in range(2):
                        b0 = q * SAMPLES + (2 * use + s) * SUB_B + m * HALF_B
                        done = act.activation(
                            gsum[:, :, b0:b0 + HALF_B].rearrange("p i b -> p b i"),
                            side[:, m, s * 256:(s + 1) * 256].rearrange("p (b i) -> p b i", i=FIELDS), ACT.Copy)
                done.then_inc(side_copied, 1)

            def copy_z3(bt, before):
                act.wait_ge(side_filled, before + 1)
                act.activation(z[:, 2, bass.ds(bt * P, P)], side[:, 0, 0:P], ACT.Copy).then_inc(side_copied, 1)

            def round_hi(groups, q, t, g):
                e = split_places(groups).index(g)
                act.wait_ge(prod_ready, groups_before(t, g) + 1)
                gone = back(groups, q < 0, g, HI, "pool", "dve")
                if gone is not None:
                    act.wait_ge(prod_used, groups_before(t, gone + 1))
                if kind_of(groups[g]) == "dve":
                    src = prod_ps[:]
                else:
                    src = prod[:, prod_slot(q, g)]
                act.activation(hi[:, e % HI], src, ACT.Copy).then_inc(hi_ready, 1)

            act.wait_ge(w1_loaded, 32)
            act.activation(w1_hi_flat, w1_whole, ACT.Copy).then_inc(w1_hi_ready, 1)
            for k in range(4):
                copy_xt(k, k)
            store_xt(0, 4)
            for c in range(N_Y):
                copy_rhs(c % RING, c % 2, 16, None if c < 2 else sum(1 for x in L0 if x[3] <= c - 2))
            copy_h1(0, 0)

            def chunk(bt, q, t):
                last = is_last(t)
                groups = groups_of(t)
                before = side_before(bt, q)

                def copy(j):
                    if j < 2:
                        done = -(N_X // PAIR) if j == 0 else 0
                    else:
                        done = sum(1 for x in groups if x[3] <= j - 2)
                    slot = (N_Y + j) % RING
                    loads = t * (16 * N_R // RING) + 16 * ((N_Y + j) // RING + 1)
                    copy_rhs(slot, j % 2, loads, groups_before(t, done))

                def side_work(g, before):
                    if g == XCOL_AT:
                        if q >= 0:
                            copy_h2(t - 1, q % 2)
                        act.wait_ge(side_filled, before + 1)
                        act.activation(xcol[:, (q + 1) % 2], side[:, 0, 0:SUB * FIELDS].rearrange("p (s f) -> p s f", s=SUB),
                                       ACT.Copy).then_inc(side_copied, 1)
                        before = before + 1
                    if g in XT_AT and makes_xt(bt, q):
                        if g == XT_AT[0]:
                            act.wait_ge(x_stored, bt * 16 + 16)
                        copy_xt(XT_AT.index(g), before)
                        before = before + 1
                        if g == XT_AT[-1]:
                            store_xt(bt + 1, before)
                    if q >= 0 and g == H2T_AT:
                        copy_h2t(before)
                        before = before + 1
                    if q >= 0 and g in G_AT:
                        copy_g(q, G_AT.index(g), before)
                        before = before + 1
                    if g == L0_END and not last:
                        copy_h1(t + 1, q % 2)
                    return before

                for g in range(len(groups)):
                    j = groups[g][3]
                    if first_of(groups, g):
                        if j == 0:
                            copy(0)
                        if j + 1 <= groups[-1][3]:
                            copy(j + 1)
                    if kind_of(groups[g]) != "raw":
                        round_hi(groups, q, t, g)
                    if g >= LAG:
                        before = side_work(g - LAG, before)
                for g in range(len(groups) - LAG, len(groups)):
                    before = side_work(g, before)
                if q == 3:
                    copy_z3(bt, before)

            each_chunk(act, chunk)
            tail = side_before(BLOCKS - 1, 2) + 4
            copy_h2(CHUNKS - 1, (CHUNKS - 1) % 2)
            copy_h2t(tail)
            for use in range(2):
                copy_g(PER_BLOCK - 1, use, tail + 1 + use)
            copy_z3(BLOCKS - 1, tail + 3)
            act.wait_ge(top_loaded, 16 * 7)
            for m in range(4):
                act.wait_ge(hid_done, m + 1)
                act.activation(hid1[:, m, :], rhs[:, m % 2, :], ACT.Relu, bias=bt1[:, m:m + 1]).then_inc(hid_copied, 1)
            for m in range(2):
                act.wait_ge(hid_done, 5 + m)
                act.activation(hid2[:, m, :], acc[:, m, :], ACT.Relu, bias=bt2[:, m:m + 1]).then_inc(hid_copied, 1)
            act.wait_ge(hid_done, 7)
            act.activation(y, side[0:1, 0, :], ACT.Copy).then_inc(hid_copied, 1)

        @block.tensor
        def _(pe):
            def side_free(before):
                pe.wait_ge(side_copied, before)
                pe.sem_inc(pe_passed, 1)

            def turn_xt(k, bt, before):
                if k == 0:
                    pe.wait_ge(rows_gathered, bt * (16 * FIELDS) + 16 * FIELDS)
                    pe.sem_inc(pe_passed, 1)
                if not isinstance(before, int) or before > 0:
                    side_free(before)
                for d in range(4):
                    last = pe.transpose(side[0:FIELDS, 0, d * P:(d + 1) * P], rows[:, :, 4 * k + d], ident[:])
                last.then_inc(side_filled, 1)

            def layer0(g, n, slot, bank):
                _, c, a, _ = L0[g]
                pe.wait_ge(prod_ready, n + 1)
                for i in range(PAIR):
                    mm = pe.matmul(acc[:, bank, :], w0[:, W0_TILES.index((c, a + i)), :], prod[:, slot, i, :],
                                   start=g == 0 and i == 0, stop=g == len(L0) - 1 and i == PAIR - 1,
                                   skip_group_check=True)
                mm.then_inc(prod_used, 1)

            def layer1(groups, q, t, g):
                _, c, a, _ = groups[g]
                kind = kind_of(groups[g])
                bank = acc[:, (q + 1) % 2, :]
                first, last = g == 0, g == len(groups) - 1
                if kind == "raw":
                    slot = prod_slot(q, g)
                    pe.wait_ge(prod_ready, groups_before(t, g) + 1)
                    for i in range(PAIR):
                        mm = pe.matmul(bank, w1_raw[:, W1_RAW[c, a + i], :], prod[:, slot, i, :],
                                       start=False, stop=last and i == PAIR - 1, skip_group_check=True)
                    mm.then_inc(prod_used, 1)
                    return
                e = split_places(groups).index(g)
                pe.wait_ge(hi_ready, t * N_SPLIT + (e + 1))
                for i in range(PAIR):
                    w = W1_SPLIT[c, a + i]
                    pe.matmul(bank, w1_hi[:, w, :], hi[:, e % HI, i, :], start=first and i == 0, stop=False,
                              skip_group_check=True)
                    pe.matmul(bank, w1_lo[:, w, :], hi[:, e % HI, i, :], start=False, stop=False,
                              skip_group_check=True)
                wait_lo(pe, kind, t, places(groups, kind).index(g))
                for i in range(PAIR):
                    mm = pe.matmul(bank, w1_hi[:, W1_SPLIT[c, a + i], :], lo[:, prod_slot(q, g), i, :], start=False,
                                   stop=last and i == PAIR - 1, skip_group_check=True)
                mm.then_inc(prod_used, 1)

            def turn_h2(before):
                pe.wait_ge(side_copied, before)
                for s in range(SUB):
                    last = pe.transpose(side[:, 0, s * P:(s + 1) * P], h2[:, s * P:(s + 1) * P], ident[:])
                last.then_inc(side_filled, 1)

            def form_g(bt, q, use, before):
                pe.wait_ge(side_copied, before)
                pe.wait_ge(xdiag_ready, bt * (PER_BLOCK * SUB) + (q * SUB + 2 * use + 2))
                for s in range(2):
                    for m in range(2):
                        half = slice(m * 64, (m + 1) * 64)
                        mm = pe.matmul(side[:, m, s * 256:(s + 1) * 256], h2t[half, 2 * use + s, :],
                                       xdiag[half, s].rearrange("p b i -> p (b i)"),
                                       start=True, stop=True, skip_group_check=True)
                mm.then_inc(side_filled, 1)

            def contract_w2(bt, k, before):
                if k == 0:
                    pe.wait_ge(side_copied, before)
                pe.wait_ge(w2_loaded[k % W2_SLOTS], bt * (16 * F_LOADS // W2_SLOTS) + 16 * (k // W2_SLOTS + 1))
                for i in range(W2_I):
                    mm = pe.matmul(side[:, 0, 0:P], w2[:, k % W2_SLOTS, i, :], gsum[:, k * W2_I + i, :],
                                   start=k == 0 and i == 0, stop=k == F_LOADS - 1 and i == W2_I - 1,
                                   skip_group_check=True)
                mm.then_inc(w2_free, 1)
                if k == F_LOADS - 1:
                    pe.drain().then_inc(side_filled, 1)

            pe.sem_inc(w2_free, W2_SLOTS)
            pe.wait_ge(consts_loaded, 32)
            for k in range(4):
                turn_xt(k, 0, k)
            pe.wait_ge(w0_summed, 1)
            for g in range(len(L0)):
                layer0(g, g, g % PROD, 0)
            pe.wait_ge(w1_lo_ready, 1)

            def chunk(bt, q, t):
                groups = groups_of(t)
                before = side_before(bt, q)
                loads = 0
                for g, (layer, c, a, j) in enumerate(groups):
                    if g == 0:
                        pe.wait_ge(h1_copied, t + 1)
                    if g == XCOL_AT:
                        side_free(before)
                        for s in range(SUB):
                            xs = xt[:, (q + 1) % 4 * SAMPLES + s * SUB_B:(q + 1) % 4 * SAMPLES + (s + 1) * SUB_B, :]
                            mm = pe.transpose(side[:, 0, s * FIELDS:(s + 1) * FIELDS], xs.rearrange("f b d -> f (b d)"),
                                              ident[0:FIELDS, 0:FIELDS])
                        mm.then_inc(side_filled, 1)
                        before = before + 1
                    if g in XT_AT and makes_xt(bt, q):
                        turn_xt(XT_AT.index(g), bt + 1, before)
                        before = before + 1
                    if q >= 0 and g == H2T_AT:
                        pe.wait_ge(h2_copied, t)
                        turn_h2(before)
                        before = before + 1
                    if q >= 0 and g in G_AT:
                        form_g(bt, q, G_AT.index(g), before)
                        before = before + 1
                    if q == 3 and g in F_AT:
                        contract_w2(bt, loads, before)
                        loads += 1
                    if layer == 0:
                        layer0(g - len(L1_A), groups_before(t, g), prod_slot(q, g), q % 2)
                    else:
                        layer1(groups, q, t, g)

            each_chunk(pe, chunk)
            pe.wait_ge(h2_copied, CHUNKS)
            tail = side_before(BLOCKS - 1, 2) + 4
            turn_h2(tail)
            for use in range(2):
                form_g(BLOCKS - 1, PER_BLOCK - 1, use, tail + 1 + use)
            for k in range(F_LOADS):
                contract_w2(BLOCKS - 1, k, tail + 3)

            pe.wait_ge(top_loaded, 16 * 7)
            pe.wait_ge(z_summed, 2 * CHUNKS)
            pe.wait_ge(side_copied, tail + 4)
            for m in range(4):
                if m >= 2:
                    pe.wait_ge(hid_copied, m - 1)
                for k in range(3):
                    pe.matmul(rhs[:, m % 2, :], wt1[:, k, m * P:(m + 1) * P], z[:, k, :], start=k == 0, stop=False)
                pe.matmul(rhs[:, m % 2, :], wt1[0:DENSE, 3, m * P:(m + 1) * P], dense,
                          start=False, stop=True).then_inc(hid_done, 1)
            for m in range(2):
                for k in range(4):
                    pe.wait_ge(hid_copied, k + 1)
                    mm = pe.matmul(acc[:, m, :], wt2[:, k, m * P:(m + 1) * P], hid1[:, k, :], start=k == 0, stop=k == 3)
                mm.then_inc(hid_done, 1)
            for k in range(2):
                pe.wait_ge(hid_copied, 5 + k)
                mm = pe.matmul(side[0:1, 0, :], wt3[:, k:k + 1], hid2[:, k, :], start=k == 0, stop=k == 1)
            mm.then_inc(hid_done, 1)


def kernel(**inputs):
    import numpy as np
    import concourse.bacc as bacc
    from concourse.bass_utils import run_bass_kernel_spmd

    f = {k: np.ascontiguousarray(np.asarray(v)) for k, v in inputs.items()}
    arrays = {f"tbl_{i}": f[f"tbl_{i}"] for i in range(FIELDS)}
    arrays["ids"] = f["ids"]
    for name in ("W_top1", "W_top2"):
        arrays[name] = f[name]
    pairs0 = f["L0_rec_W0"].reshape(FIELDS, FIELDS, NF)
    there, back = [], []
    for c, a in W0_TILES:
        i, j = slice(a * XA, (a + 1) * XA), slice(c * RB, (c + 1) * RB)
        there.append(pairs0[i, j].reshape(P, NF))
        other = pairs0[j, i].transpose(1, 0, 2).reshape(P, NF)
        back.append(other if a < 2 * c else np.zeros_like(other))
    arrays["w0_tiles"] = np.ascontiguousarray(np.stack([np.stack(there, 1), np.stack(back, 1)]))
    pairs1 = f["L0_rec_W1"].reshape(N_X, XA, N_H, RB, NF)
    w1_tiles = pairs1.transpose(1, 3, 2, 0, 4).reshape(P, N_H, N_X, NF)
    arrays["w1_split"] = np.ascontiguousarray(np.concatenate([w1_tiles[:, c, a] for c, a in W1_SPLIT], 1))
    arrays["w1_raw"] = np.ascontiguousarray(np.stack([w1_tiles[:, c, a] for c, a in W1_RAW], 1))
    arrays["w2_rows"] = np.ascontiguousarray(f["L0_rec_W2"].reshape(FIELDS, NF, NF).transpose(1, 0, 2))
    arrays["w_top3_cols"] = np.ascontiguousarray(f["W_top3"].reshape(2, P).T)
    arrays["b_top1_cols"] = np.ascontiguousarray(f["b_top1"].reshape(4, P).T)
    arrays["b_top2_cols"] = np.ascontiguousarray(f["b_top2"].reshape(2, P).T)
    arrays["dense_rows"] = np.ascontiguousarray(f["dense_ctx"].T)
    arrays["identity"] = np.eye(P, dtype=np.float32)
    arrays["sample_mask"] = np.ascontiguousarray(np.tile(np.kron(np.eye(HALF_B), np.ones((DIM, 1))), (2, 1)).astype(np.float32))

    nc = bacc.Bacc("TRN2", target_bir_lowering=False, num_devices=1)
    ins = {k: nc.dram_tensor(k, a.shape, mybir.dt.from_np(a.dtype), kind="ExternalInput").ap() for k, a in arrays.items()}
    out = nc.dram_tensor("out", (BATCH, 1), F32, kind="ExternalOutput").ap()
    build(nc, ins, out)
    r = run_bass_kernel_spmd(nc, [arrays], core_ids=[0])
    return r.results[0]["out"]
```

```python
from contextlib import ExitStack

import concourse.bass as bass
from concourse import mybir

F32 = mybir.dt.float32
F32R = mybir.dt.float32r
I32 = mybir.dt.int32
U32 = mybir.dt.uint32
ALU = mybir.AluOpType
ACT = mybir.ActivationFunctionType
AX_X = mybir.AxisListType.X

P = 128
FIELDS, DIM, BATCH = 64, 16, 512
NF = 128
CH = 512
SAMPLES = CH // DIM
CHUNKS = BATCH * DIM // CH
PER_BLOCK = P // SAMPLES
BLOCKS = CHUNKS // PER_BLOCK
XA, RB = 8, 16
N_X = FIELDS // XA
N_Y = FIELDS // RB
N_H = NF // RB
PAIR = 2
SUB = CH // P
SUB_B = P // DIM
HALF_B = SUB_B // 2
RING = 4
PROD = 6
HI = 3
LAG = 2
W1_PARTS = 8
W2_I, W2_SLOTS = 4, 2
STEP_F = P // SAMPLES
STEPS = FIELDS // STEP_F
QUARTERS = N_Y
W2_IN_PROD = 3
HIDDEN1, HIDDEN2, DENSE = 512, 256, 16

ORDER = [(1, 0), (1, 1), (1, 2), (1, 3), (1, 4), (1, 5), (0, 0), (0, 1), (0, 2), (0, 3), (1, 6), (1, 7)]


def groups_for(order):
    return [(layer, c, a, j) for j, (layer, c) in enumerate(order)
            for a in range(0, N_X if layer else 2 * c + 2, PAIR)]


L0 = groups_for([(0, c) for c in range(N_Y)])
GROUPS = groups_for(ORDER)
GROUPS_LAST = groups_for([x for x in ORDER if x[0]])
L0_AT = [g for g, x in enumerate(GROUPS) if x[0] == 0]
L0_END = L0_AT[-1] + 1
N_G, N_R = len(GROUPS), N_Y + N_H
W0_TILES = [(c, a) for c in range(N_Y) for a in range(2 * c + 2)]
W2_PROD_AT = W2_SLOTS * W2_I + len(W0_TILES)
W2_PROD_I = (FIELDS - W2_PROD_AT) // W2_IN_PROD
assert W2_PROD_I * W2_IN_PROD == FIELDS - W2_PROD_AT <= PROD * PAIR * CH // NF
W0_BACK = [(c, a) for c, a in W0_TILES if a < 2 * c]


def quarter(k):
    return slice(k * STEPS // QUARTERS, (k + 1) * STEPS // QUARTERS)


KINDS = ("pool", "dve", "pool", "raw")
assert KINDS[-1] != "dve"


def kind_of(group):
    layer, _, a, _ = group
    return KINDS[a // PAIR] if layer else "raw"


def places(groups, *kinds):
    return [g for g, x in enumerate(groups) if kind_of(x) in kinds]


def split_places(groups):
    return places(groups, "pool", "dve")


N_SPLIT, N_POOL, N_DVE = (len(places(GROUPS, *k)) for k in (("pool", "dve"), ("pool",), ("dve",)))
W1_SPLIT = {(c, a + i): n for n, (c, a, i) in enumerate(
    (c, a, i) for c in range(N_H) for a in range(0, N_X, PAIR) if KINDS[a // PAIR] != "raw" for i in range(PAIR))}
W1_RAW = {(c, a + i): n for n, (c, a, i) in enumerate(
    (c, a, i) for c in range(N_H) for a in range(0, N_X, PAIR) if KINDS[a // PAIR] == "raw" for i in range(PAIR))}

XCOL_AT = 0
H2T_AT = 4
G_AT = (8, 12)
F_LOADS = FIELDS // W2_I
F_AT = tuple(16 + 3 * k // 2 for k in range(F_LOADS))
X_LOADS_AT = 5
H1_SUM_AT = L0_END + 6
X_STORE_AT = 38
RHS_LEAD = 8
NEXT_H_AT = L0_END + 4


def first_of(groups, g):
    return g == 0 or groups[g - 1][3] != groups[g][3]


def first_place(groups, j):
    return next(g for g, x in enumerate(groups) if x[3] == j)


def groups_before(t, g):
    return t * N_G + (len(L0) + g)


def rhs_before(t, j):
    return t * N_R + (N_Y + j)


def prod_slot(q, g):
    return (len(L0) + N_G * (q + 1) + g) % PROD


assert PER_BLOCK * N_G % PROD == 0 and N_SPLIT % HI == 0


def back(groups, start, g, depth, *kinds):
    here = places(groups, *kinds)
    ahead = L0 if start else GROUPS
    there = [x - len(ahead) for x in places(ahead, *kinds)]
    every = there + here
    at = every.index(g) - depth
    return every[at] if at >= 0 else None


def side_before(bt, q):
    if q < 0:
        return 0
    return bt * (4 * PER_BLOCK + 1) + (1 + 4 * q)


def build(nc, ins, out):
    with ExitStack() as ctx:
        def sb(name, shape, dt=F32):
            return ctx.enter_context(nc.sbuf_tensor(f"{name}_sb", shape, dt))

        def psum(name, shape):
            return ctx.enter_context(nc.psum_tensor(name, shape, F32))

        def sem(name):
            return ctx.enter_context(nc.semaphore(name))

        x_dram = nc.dram_tensor("x_scratch", [CHUNKS, FIELDS, CH], F32, kind="Internal").ap()
        h1_dram = nc.dram_tensor("h1_scratch", [NF, CHUNKS * CH], F32, kind="Internal").ap()

        ident = sb("ident", [P, P])
        mask = sb("mask", [P, HALF_B])
        w0 = sb("w0", [P, len(W0_TILES), NF])
        w1_raw = sb("w1_raw", [P, len(W1_RAW), NF])
        w1_hi = sb("w1_hi", [P, len(W1_SPLIT), NF], F32R)
        w1_lo = sb("w1_lo", [P, len(W1_SPLIT), NF], F32R)
        w2 = sb("w2", [P, W2_SLOTS, W2_I, NF])
        ids = sb("ids", [P, CHUNKS, STEPS], I32)
        table_rows = sb("table_rows", [P, STEPS], I32)
        rows_now = sb("rows_now", [P, STEPS], I32)
        rows = sb("rows", [P, 2, STEPS, DIM])
        xt = sb("xt", [FIELDS, CH])
        x_tiles = sb("x_tiles", [P, 2, N_X, CH])
        rhs_ring = sb("rhs_ring", [P, RING, CH])
        hi = sb("hi", [P, HI, PAIR, CH], F32R)
        ring_at = -(-nc.sbuf_base // 32) * 32
        sb("prod_space", [P, PROD, PAIR, CH])
        prod = nc.alloc_sbuf_tensor_at("prod_sb", [P, PROD, PAIR, CH], F32, offset=ring_at)
        lo = nc.alloc_sbuf_tensor_at("lo_sb", [P, PROD, PAIR, CH], F32R, offset=ring_at)
        h1 = sb("h1", [NF, CH])
        h2 = sb("h2", [NF, CH])
        h2t = sb("h2t", [P, SUB, NF])
        xcol = sb("xcol", [P, 2, SUB, FIELDS])
        xdiag = sb("xdiag", [P, 2, HALF_B, FIELDS])
        gsum = sb("gsum", [NF, FIELDS, P])
        z = sb("z", [NF, 3, BATCH])
        w2_in_prod = prod[:].rearrange("p s a n -> p (s a n)")[:, 0:(FIELDS - W2_PROD_AT) * NF].rearrange("p (i n) -> p i n", n=NF)
        w0_back = x_tiles[:, 1].rearrange("p a n -> p (a n)")[:, 0:len(W0_BACK) * NF]
        w1_whole = gsum[:].rearrange("p i b -> p (i b)")[:, 0:len(W1_SPLIT) * NF]
        w1_parts = [slice(k * len(W1_SPLIT) * NF // W1_PARTS, (k + 1) * len(W1_SPLIT) * NF // W1_PARTS) for k in range(W1_PARTS)]
        w1_hi_flat = w1_hi[:].rearrange("p k n -> p (k n)")
        w1_lo_flat = w1_lo[:].rearrange("p k n -> p (k n)")
        top = x_tiles[:, 0].rearrange("p a n -> p (a n)")
        wt1 = top[:, 0:4 * HIDDEN1].rearrange("p (k n) -> p k n", k=4)
        wt2 = top[:, 2048:2048 + 4 * HIDDEN2].rearrange("p (k n) -> p k n", k=4)
        wt3 = top[:, 3072:3072 + 2]
        bt1 = top[:, 3080:3084]
        bt2 = top[:, 3088:3090]
        dense = top[0:DENSE, 3584:3584 + BATCH]
        hid1 = x_tiles[:, 1, 0:4, :]
        hid2 = x_tiles[:, 1, 4:6, :]
        y = x_tiles[0:1, 1, 6, :]

        acc = psum("acc", [P, 2, CH])
        rhs = psum("rhs", [P, 2, CH])
        prod_ps = psum("prod_ps", [P, PAIR, CH])
        side = psum("side", [P, 2, CH])

        hid1_ps = [rhs[:, 0, :], rhs[:, 1, :], prod_ps[:, 0, :], prod_ps[:, 1, :]]

        ids_loaded = sem("ids_loaded")
        consts_loaded = sem("consts_loaded")
        w0_loaded = sem("w0_loaded")
        w0_summed = sem("w0_summed")
        w1_loaded = [sem(f"w1_loaded{k}") for k in range(W1_PARTS)]
        w1_raw_loaded = sem("w1_raw_loaded")
        w1_hi_ready = sem("w1_hi_ready")
        w1_lo_ready = sem("w1_lo_ready")
        w2_loaded = [sem(f"w2_loaded{k}") for k in range(W2_SLOTS)]
        w2_free = sem("w2_free")
        w2_in_w0_loaded = sem("w2_in_w0_loaded")
        w2_in_prod_loaded = [sem(f"w2_in_prod_loaded{k}") for k in range(W2_IN_PROD)]
        top_loaded = sem("top_loaded")
        rows_known = sem("rows_known")
        first_gathered = [sem(f"first_gathered{k}") for k in range(QUARTERS)]
        rows_gathered = sem("rows_gathered")
        first_stored = [sem(f"first_stored{k}") for k in range(QUARTERS)]
        x_stored = sem("x_stored")
        x_first_loaded = [sem(f"x_first_loaded{k}") for k in range(QUARTERS)]
        xt_loaded = sem("xt_loaded")
        x_loaded = [sem(f"x_loaded{k}") for k in range(2)]
        rhs_loaded = [sem(f"rhs_loaded{k}") for k in range(RING)]
        rhs_ready = sem("rhs_ready")
        prod_ready = sem("prod_ready")
        hi_ready = sem("hi_ready")
        lo_pool_ready = sem("lo_pool_ready")
        lo_dve_ready = sem("lo_dve_ready")
        prod_used = sem("prod_used")
        h1_copied = sem("h1_copied")
        h1_stored = sem("h1_stored")
        h2_copied = sem("h2_copied")
        side_filled = sem("side_filled")
        side_copied = sem("side_copied")
        xdiag_ready = sem("xdiag_ready")
        z_summed = sem("z_summed")
        hid_done = sem("hid_done")
        hid_copied = sem("hid_copied")
        y_stored = sem("y_stored")
        pe_passed = sem("pe_passed")
        pool_passed = sem("pool_passed")

        block = ctx.enter_context(nc.Block())

        def each_chunk(eng, chunk):
            chunk(0, -1, 0)
            with eng.Fori(0, BLOCKS - 1) as bt:
                for q in range(PER_BLOCK):
                    chunk(bt, q, bt * PER_BLOCK + (q + 1))
            for q in range(PER_BLOCK - 1):
                chunk(BLOCKS - 1, q, (BLOCKS - 1) * PER_BLOCK + q + 1)

        def is_last(t):
            return isinstance(t, int) and t == CHUNKS - 1

        def groups_of(t):
            return GROUPS_LAST if is_last(t) else GROUPS

        def gathers(t):
            return not isinstance(t, int) or t + 2 < CHUNKS

        def wait_lo(eng, kind, t, index):
            if kind == "pool":
                eng.wait_ge(lo_pool_ready, t * N_POOL + (index + 1))
            else:
                eng.wait_ge(lo_dve_ready, t * N_DVE + (index + 1))

        def x_of(t):
            return x_dram[bass.ds(t, 1)].rearrange("o f n -> (o f) n")

        def x_tile_rows(a, t):
            src = x_of(t)[a * XA:(a + 1) * XA, :]
            return src.unsqueeze(1).to_broadcast([XA, RB, CH])

        def load_rhs(eng, slot, src):
            rep = src.unsqueeze(0).to_broadcast([XA, RB, CH])
            eng.dma_start(rhs_ring[:, slot, :], rep).then_inc(rhs_loaded[slot], 16)

        @block.sync
        def _(sp):
            def load_x(t, par):
                for a in range(N_X):
                    sp.dma_start(x_tiles[:, par, a, :], x_tile_rows(a, t)).then_inc(x_loaded[par], 16)

            def load_xt(t):
                sp.dma_start(xt[:], x_of(t)).then_inc(xt_loaded, 16)

            def store_rows(t, slot, steps, stored):
                dst = x_of(t)[STEP_F * steps.start:STEP_F * steps.stop, :]
                sp.dma_start(dst.rearrange("(s f) (b d) -> (f b) s d", f=STEP_F, d=DIM), rows[:, slot, steps, :]).then_inc(stored, 16)

            sp.dma_start(ids[:], ins["ids_steps"]).then_inc(ids_loaded, 16)
            sp.dma_start(table_rows[:], ins["table_rows"]).then_inc(ids_loaded, 16)
            sp.dma_start(w0[:], ins["w0_tiles"]).then_inc(w0_loaded, 16)
            sp.dma_start(w0_back, ins["w0_back"]).then_inc(w0_loaded, 16)

            def load_w1(k):
                sp.dma_start(w1_whole[:, w1_parts[k]], ins["w1_split"][:, w1_parts[k]]).then_inc(w1_loaded[k], 16)

            for k in range(QUARTERS):
                sp.wait_ge(first_gathered[k], 16 * STEPS // QUARTERS)
                store_rows(0, 0, quarter(k), first_stored[k])
                if k:
                    load_w1(k - 1)
            sp.wait_ge(x_first_loaded[QUARTERS - 1], 16 * N_X // QUARTERS)
            for k in range(QUARTERS - 1, W1_PARTS):
                load_w1(k)
            sp.dma_start(w1_raw[:], ins["w1_raw"]).then_inc(w1_raw_loaded, 16)
            for k in range(QUARTERS):
                sp.wait_ge(first_stored[k], 16)
            load_xt(0)
            sp.dma_start(ident[:], ins["identity"]).then_inc(consts_loaded, 16)
            sp.dma_start(mask[:], ins["sample_mask"]).then_inc(consts_loaded, 16)
            sp.wait_ge(rows_gathered, 16 * STEPS)
            store_rows(1, 1, slice(0, STEPS), x_stored)

            def w2_load(bt, k):
                sp.wait_ge(w2_free, bt * F_LOADS + (k + 1))
                sp.dma_start(w2[:, k % W2_SLOTS], ins["w2_rows"][:, k * W2_I:(k + 1) * W2_I, :]).then_inc(
                    w2_loaded[k % W2_SLOTS], 16)

            def load_place(q, t, j, last=False):
                if not (q < 0 and N_Y + j < RING):
                    sp.wait_ge(rhs_ready, rhs_before(t, j - (RING - 1)))
                layer, c = next((x[0], x[1]) for x in (GROUPS_LAST if last else GROUPS) if x[3] == j)
                source = h1_dram[:, bass.ds(t * CH, CH)] if layer else x_of(t + 1)
                load_rhs(sp, (N_Y + j) % RING, source[c * RB:(c + 1) * RB, :])

            def first_places(t, q):
                sp.wait_ge(h1_stored, t * 16 + 16)
                for j in range(2):
                    load_place(q, t, j)

            first_places(0, -1)

            def chunk(bt, q, t):
                last = is_last(t)
                w2_done = 0
                for g in range(len(groups_of(t))):
                    if g == X_LOADS_AT:
                        sp.wait_ge(prod_ready, groups_before(t, 0))
                        if q < 0:
                            sp.wait_ge(w0_summed, N_Y - 1)
                        if not last:
                            sp.wait_ge(x_stored, t * 16 + 16)
                            load_x(t + 1, q % 2)
                            sp.wait_ge(side_copied, side_before(bt, q) + 1)
                            load_xt(t + 1)
                        else:
                            for dst, src in (
                                (wt1[:, 0:3, :], ins["W_top1"][0:3 * P, :].rearrange("(k p) n -> p k n", p=P)),
                                (wt1[0:DENSE, 3, :], ins["W_top1"][3 * P:3 * P + DENSE, :]),
                                (wt2, ins["W_top2"].rearrange("(k p) n -> p k n", p=P)),
                                (wt3, ins["w_top3_cols"]), (bt1, ins["b_top1_cols"]),
                                (bt2, ins["b_top2_cols"]), (dense, ins["dense_rows"]),
                            ):
                                sp.dma_start(dst, src).then_inc(top_loaded, 16)
                            sp.wait_ge(prod_used, groups_before(t, 0))
                            sp.dma_start(w0[:], ins["w2_rows"][:, W2_SLOTS * W2_I:W2_PROD_AT, :]).then_inc(w2_in_w0_loaded, 16)
                    for j in range(2, N_H if last else N_R):
                        start = first_place(groups_of(t), j)
                        earliest = 0 if groups_of(t)[start][0] else X_LOADS_AT
                        if g == max(start - RHS_LEAD, earliest):
                            load_place(q, t, j, last)
                    while q == 3 and w2_done < F_LOADS and F_AT[max(w2_done - W2_SLOTS, 0)] < g:
                        w2_load(bt, w2_done)
                        w2_done += 1
                    if g == X_STORE_AT and gathers(t):
                        sp.wait_ge(rows_gathered, t * (16 * STEPS) + 16 * STEPS * 2)
                        store_rows(t + 2, (q + 1) % 2, slice(0, STEPS), x_stored)
                    if g == NEXT_H_AT and not last:
                        first_places(t + 1, (q + 1) % PER_BLOCK)
                for k in range(w2_done, F_LOADS if q == 3 else 0):
                    w2_load(bt, k)

            each_chunk(sp, chunk)
            for k in range(W2_SLOTS):
                w2_load(BLOCKS - 1, k)
            sp.wait_ge(prod_used, groups_before(CHUNKS - 1, len(GROUPS_LAST)))
            for k in range(W2_IN_PROD):
                part = slice(k * W2_PROD_I, (k + 1) * W2_PROD_I)
                rows_of = slice(W2_PROD_AT + part.start, W2_PROD_AT + part.stop)
                sp.dma_start(w2_in_prod[:, part, :], ins["w2_rows"][:, rows_of, :]).then_inc(w2_in_prod_loaded[k], 16)
            sp.wait_ge(hid_copied, 7)
            sp.dma_start(out.rearrange("b o -> o b"), y).then_inc(y_stored, 16)
            sp.wait_ge(y_stored, 16)

        @block.gpsimd
        def _(pool):
            def gather(t, slot, k, gathered):
                if k == 0:
                    pool.tensor_tensor(rows_now[:], ids[:, bass.ds(t, 1), :].rearrange("p o s -> p (o s)"),
                                       table_rows[:], ALU.add).then_inc(rows_known, 1)
                    pool.wait_ge(rows_known, t + 1)
                    pool.sem_inc(pool_passed, 1)
                for s in range(STEPS)[quarter(k)]:
                    pool.indirect_dma_start(
                        rows[:, slot, s, :], None, ins["tables"],
                        bass.IndirectOffsetOnAxis(ap=rows_now[:, s:s + 1].bitcast(U32), axis=0),
                    ).then_inc(gathered, 16)

            def diagonal(bt, q, half):
                for s in range(2 * half, 2 * half + 2):
                    src = xcol[:, q % 2, s, :].unsqueeze(1).to_broadcast([P, HALF_B, FIELDS])
                    on = mask[:].unsqueeze(2).to_broadcast([P, HALF_B, FIELDS])
                    pool.tensor_tensor(xdiag[:, s % 2], src, on, ALU.mult).then_inc(xdiag_ready, 1)

            def chunk(bt, q, t):
                groups = groups_of(t)
                before = side_before(bt, q)
                g_uses = before + 2
                for g, x in enumerate(groups):
                    if g == 0 and q >= 0:
                        pool.wait_ge(side_copied, before)
                        diagonal(bt, q, 0)
                    if g == G_AT[0] + 1 and q >= 0:
                        pool.wait_ge(side_filled, g_uses + 1)
                        diagonal(bt, q, 1)
                    if x[0] == 0 and first_of(groups, g) and gathers(t):
                        if x[1] == 0:
                            pool.wait_ge(rows_gathered, t * (16 * STEPS) + 16 * STEPS)
                            if q < 0:
                                for k in range(QUARTERS):
                                    pool.wait_ge(first_stored[k], 16)
                            else:
                                pool.wait_ge(x_stored, t * 16)
                        gather(t + 2, (q + 1) % 2, x[1], rows_gathered)
                    if kind_of(x) == "pool":
                        subtract(groups, q, t, g)

            def subtract(groups, q, t, g):
                e, slot = split_places(groups).index(g), prod_slot(q, g)
                pool.wait_ge(hi_ready, t * N_SPLIT + (e + 1))
                pool.tensor_tensor(lo[:, slot], prod[:, slot], hi[:, e % HI].bitcast(F32),
                                   ALU.subtract).then_inc(lo_pool_ready, 1)

            pool.wait_ge(ids_loaded, 32)
            for k in range(QUARTERS):
                gather(0, 0, k, first_gathered[k])
            for k in range(QUARTERS):
                pool.wait_ge(first_gathered[k], 16 * STEPS // QUARTERS)
            for k in range(QUARTERS):
                gather(1, 1, k, rows_gathered)
            pool.wait_ge(consts_loaded, 32)
            each_chunk(pool, chunk)
            pool.wait_ge(side_copied, side_before(BLOCKS - 1, 2) + 4)
            diagonal(BLOCKS - 1, 3, 0)
            pool.wait_ge(side_filled, side_before(BLOCKS - 1, 2) + 4 + 2)
            diagonal(BLOCKS - 1, 3, 1)

        @block.vector
        def _(dve):
            dve.wait_ge(w0_loaded, 32)
            for c in range(1, N_Y):
                there = w0[:, W0_TILES.index((c, 0)):W0_TILES.index((c, 2 * c)), :].rearrange("p t n -> p (t n)")
                at = W0_BACK.index((c, 0)) * NF
                dve.tensor_tensor(there, there, w0_back[:, at:at + 2 * c * NF], ALU.add).then_inc(w0_summed, 1)

            def split_w1(k):
                dve.wait_ge(w1_hi_ready, k + 1)
                dve.tensor_tensor(w1_lo_flat[:, w1_parts[k]], w1_whole[:, w1_parts[k]],
                                  w1_hi_flat[:, w1_parts[k]].bitcast(F32), ALU.subtract).then_inc(w1_lo_ready, 1)

            def operands(par, a, bank):
                return x_tiles[:, par, a:a + PAIR, :], rhs[:, bank:bank + 1, :].to_broadcast([P, PAIR, CH])

            def sum_over_d(layer, src, t):
                dve.tensor_reduce(
                    z[:, layer, bass.ds(t * SAMPLES, SAMPLES)], src[:].rearrange("p (b d) -> p b d", d=DIM),
                    AX_X, ALU.add).then_inc(z_summed, 1)

            for g, (_, c, a, j) in enumerate(L0):
                if first_of(L0, g):
                    dve.wait_ge(rhs_ready, j + 1)
                    dve.wait_ge(x_first_loaded[c], 16 * N_X // QUARTERS)
                if g >= PROD:
                    dve.wait_ge(prod_used, g - (PROD - 1))
                dve.tensor_tensor(prod[:, g % PROD], *operands(0, a, j % 2), ALU.mult).then_inc(prod_ready, 1)
            for k in range(W1_PARTS // 2):
                split_w1(k)
            dve.wait_ge(h1_copied, 1)
            sum_over_d(0, h1, 0)
            for k in range(W1_PARTS // 2, W1_PARTS):
                split_w1(k)

            def product(groups, bt, q, t, g):
                layer, c, a, j = groups[g]
                kind = kind_of(groups[g])
                if first_of(groups, g):
                    dve.wait_ge(rhs_ready, rhs_before(t, j) + 1)
                if layer == 0 and g == L0_AT[0]:
                    dve.wait_ge(x_loaded[q % 2], 16 * N_X if q < 0 else bt * (32 * N_X) + 16 * N_X * (1 + (q + 1) // 2))
                par = (q + 1) % 2 if layer else q % 2
                if kind == "dve":
                    d = places(groups, "dve").index(g)
                    if q >= 0 or d > 0:
                        dve.wait_ge(lo_dve_ready, t * N_DVE + d)
                    dve.tensor_tensor(prod_ps[:], *operands(par, a, j % 2), ALU.mult).then_inc(prod_ready, 1)
                    return
                wait_slot(t, g)
                dve.tensor_tensor(prod[:, prod_slot(q, g)], *operands(par, a, j % 2), ALU.mult).then_inc(prod_ready, 1)

            def wait_slot(t, g):
                dve.wait_ge(prod_used, groups_before(t, g - (PROD - 1)))

            def subtract(groups, q, t, g):
                e = split_places(groups).index(g)
                dve.wait_ge(hi_ready, t * N_SPLIT + (e + 1))
                wait_slot(t, g)
                dve.tensor_tensor(lo[:, prod_slot(q, g)], prod_ps[:], hi[:, e % HI].bitcast(F32),
                                  ALU.subtract).then_inc(lo_dve_ready, 1)

            def chunk(bt, q, t):
                last = is_last(t)
                groups = groups_of(t)
                for g in range(len(groups)):
                    if g == 8 and q >= 0:
                        dve.wait_ge(h2_copied, t)
                        sum_over_d(1, h2, t - 1)
                    if g == H1_SUM_AT and not last:
                        dve.wait_ge(h1_copied, t + 2)
                        sum_over_d(0, h1, t + 1)
                    product(groups, bt, q, t, g)
                    if g > 0 and kind_of(groups[g - 1]) == "dve":
                        subtract(groups, q, t, g - 1)

            each_chunk(dve, chunk)
            dve.wait_ge(h2_copied, CHUNKS)
            sum_over_d(1, h2, CHUNKS - 1)

        @block.scalar
        def _(act):
            def copy_rhs(slot, bank, loads, free):
                act.wait_ge(rhs_loaded[slot], loads)
                if free is not None:
                    act.wait_ge(prod_ready, free)
                act.activation(rhs[:, bank, :], rhs_ring[:, slot, :], ACT.Copy).then_inc(rhs_ready, 1)

            def copy_h1(t, bank):
                first = isinstance(t, int) and t == 0
                act.wait_ge(prod_used, len(L0) if first else groups_before(t, L0_END - N_G))
                if not first:
                    act.wait_ge(h1_stored, t * 16)
                    act.wait_ge(z_summed, 1 if isinstance(t, int) and t == 1 else t * 2 - 2)
                act.activation(h1[:], acc[:, bank, :], ACT.Copy).then_inc(h1_copied, 1)
                act.wait_ge(h1_copied, t + 1)
                act.dma_start(h1_dram[:, bass.ds(t * CH, CH)], h1[:]).then_inc(h1_stored, 16)

            def copy_h2(t, bank):
                act.wait_ge(prod_used, groups_before(t + 1, 0) - (len(L0) if is_last(t) else 0))
                act.activation(h2[:], acc[:, bank, :], ACT.Copy).then_inc(h2_copied, 1)

            def copy_h2t(before):
                act.wait_ge(side_filled, before + 1)
                act.activation(h2t[:].rearrange("p s n -> p (s n)"), side[:, 0, :], ACT.Copy).then_inc(side_copied, 1)

            def copy_g(q, use, before):
                act.wait_ge(side_filled, before + 1)
                for m in range(2):
                    for s in range(2):
                        b0 = q * SAMPLES + (2 * use + s) * SUB_B + m * HALF_B
                        done = act.activation(
                            gsum[:, :, b0:b0 + HALF_B].rearrange("p i b -> p b i"),
                            side[:, m, s * 256:(s + 1) * 256].rearrange("p (b i) -> p b i", i=FIELDS), ACT.Copy)
                done.then_inc(side_copied, 1)

            def copy_z3(bt, before):
                act.wait_ge(side_filled, before + 1)
                act.activation(z[:, 2, bass.ds(bt * P, P)], side[:, 0, 0:P], ACT.Copy).then_inc(side_copied, 1)

            def round_hi(groups, q, t, g):
                e = split_places(groups).index(g)
                act.wait_ge(prod_ready, groups_before(t, g) + 1)
                gone = back(groups, q < 0, g, HI, "pool", "dve")
                if gone is not None:
                    act.wait_ge(prod_used, groups_before(t, gone + 1))
                if kind_of(groups[g]) == "dve":
                    src = prod_ps[:]
                else:
                    src = prod[:, prod_slot(q, g)]
                act.activation(hi[:, e % HI], src, ACT.Copy).then_inc(hi_ready, 1)

            def first_x(k):
                act.wait_ge(first_stored[k], 16)
                for a in range(k * N_X // QUARTERS, (k + 1) * N_X // QUARTERS):
                    act.dma_start(x_tiles[:, 0, a, :], x_tile_rows(a, 0)).then_inc(x_first_loaded[k], 16)
                load_rhs(act, k % RING, x_dram[0, k * RB:(k + 1) * RB, :])

            def round_w1(k):
                act.wait_ge(w1_loaded[k], 16)
                act.activation(w1_hi_flat[:, w1_parts[k]], w1_whole[:, w1_parts[k]], ACT.Copy).then_inc(w1_hi_ready, 1)

            for c in range(N_Y):
                first_x(c)
                copy_rhs(c % RING, c % 2, 16, None if c < 2 else sum(1 for x in L0 if x[3] <= c - 2))
            for k in range(W1_PARTS // 2):
                round_w1(k)
            copy_h1(0, 0)
            for k in range(W1_PARTS // 2, W1_PARTS):
                round_w1(k)

            def chunk(bt, q, t):
                last = is_last(t)
                groups = groups_of(t)
                before = side_before(bt, q)

                def copy(j):
                    if j < 2:
                        done = -(N_X // PAIR) if j == 0 else 0
                    else:
                        done = sum(1 for x in groups if x[3] <= j - 2)
                    slot = (N_Y + j) % RING
                    loads = t * (16 * N_R // RING) + 16 * ((N_Y + j) // RING + 1)
                    copy_rhs(slot, j % 2, loads, groups_before(t, done))

                def side_work(g, before):
                    if g == XCOL_AT:
                        if q >= 0:
                            copy_h2(t - 1, q % 2)
                        act.wait_ge(side_filled, before + 1)
                        act.activation(xcol[:, (q + 1) % 2], side[:, 0, 0:SUB * FIELDS].rearrange("p (s f) -> p s f", s=SUB),
                                       ACT.Copy).then_inc(side_copied, 1)
                        before = before + 1
                    if q >= 0 and g == H2T_AT:
                        copy_h2t(before)
                        before = before + 1
                    if q >= 0 and g in G_AT:
                        copy_g(q, G_AT.index(g), before)
                        before = before + 1
                    if g == L0_END and not last:
                        copy_h1(t + 1, q % 2)
                    return before

                for g in range(len(groups)):
                    j = groups[g][3]
                    if first_of(groups, g):
                        if j == 0:
                            copy(0)
                        if j + 1 <= groups[-1][3]:
                            copy(j + 1)
                    if kind_of(groups[g]) != "raw":
                        round_hi(groups, q, t, g)
                    if g >= LAG:
                        before = side_work(g - LAG, before)
                for g in range(len(groups) - LAG, len(groups)):
                    before = side_work(g, before)
                if q == 3:
                    copy_z3(bt, before)

            each_chunk(act, chunk)
            tail = side_before(BLOCKS - 1, 2) + 4
            copy_h2(CHUNKS - 1, (CHUNKS - 1) % 2)
            copy_h2t(tail)
            for use in range(2):
                copy_g(PER_BLOCK - 1, use, tail + 1 + use)
            copy_z3(BLOCKS - 1, tail + 3)
            act.wait_ge(top_loaded, 16 * 7)
            for m in range(4):
                act.wait_ge(hid_done, m + 1)
                act.activation(hid1[:, m, :], hid1_ps[m], ACT.Relu, bias=bt1[:, m:m + 1]).then_inc(hid_copied, 1)
            for m in range(2):
                act.wait_ge(hid_done, 5 + m)
                act.activation(hid2[:, m, :], acc[:, m, :], ACT.Relu, bias=bt2[:, m:m + 1]).then_inc(hid_copied, 1)
            act.wait_ge(hid_done, 7)
            act.activation(y, side[0:1, 0, :], ACT.Copy).then_inc(hid_copied, 1)

        @block.tensor
        def _(pe):
            def layer0(g, n, slot, bank):
                _, c, a, _ = L0[g]
                pe.wait_ge(prod_ready, n + 1)
                for i in range(PAIR):
                    mm = pe.matmul(acc[:, bank, :], w0[:, W0_TILES.index((c, a + i)), :], prod[:, slot, i, :],
                                   start=g == 0 and i == 0, stop=g == len(L0) - 1 and i == PAIR - 1,
                                   skip_group_check=True)
                mm.then_inc(prod_used, 1)

            def layer1(groups, q, t, g):
                _, c, a, _ = groups[g]
                kind = kind_of(groups[g])
                bank = acc[:, (q + 1) % 2, :]
                first, last = g == 0, g == len(groups) - 1
                if kind == "raw":
                    slot = prod_slot(q, g)
                    pe.wait_ge(prod_ready, groups_before(t, g) + 1)
                    for i in range(PAIR):
                        mm = pe.matmul(bank, w1_raw[:, W1_RAW[c, a + i], :], prod[:, slot, i, :],
                                       start=False, stop=last and i == PAIR - 1, skip_group_check=True)
                    mm.then_inc(prod_used, 1)
                    return
                e = split_places(groups).index(g)
                pe.wait_ge(hi_ready, t * N_SPLIT + (e + 1))
                for i in range(PAIR):
                    w = W1_SPLIT[c, a + i]
                    pe.matmul(bank, w1_hi[:, w, :], hi[:, e % HI, i, :], start=first and i == 0, stop=False,
                              skip_group_check=True)
                    pe.matmul(bank, w1_lo[:, w, :], hi[:, e % HI, i, :], start=False, stop=False,
                              skip_group_check=True)
                wait_lo(pe, kind, t, places(groups, kind).index(g))
                for i in range(PAIR):
                    mm = pe.matmul(bank, w1_hi[:, W1_SPLIT[c, a + i], :], lo[:, prod_slot(q, g), i, :], start=False,
                                   stop=last and i == PAIR - 1, skip_group_check=True)
                mm.then_inc(prod_used, 1)

            def turn_h2(before):
                pe.wait_ge(side_copied, before)
                for s in range(SUB):
                    last = pe.transpose(side[:, 0, s * P:(s + 1) * P], h2[:, s * P:(s + 1) * P], ident[:])
                last.then_inc(side_filled, 1)

            def form_g(bt, q, use, before):
                pe.wait_ge(side_copied, before)
                pe.wait_ge(xdiag_ready, bt * (PER_BLOCK * SUB) + (q * SUB + 2 * use + 2))
                for s in range(2):
                    for m in range(2):
                        half = slice(m * 64, (m + 1) * 64)
                        mm = pe.matmul(side[:, m, s * 256:(s + 1) * 256], h2t[half, 2 * use + s, :],
                                       xdiag[half, s].rearrange("p b i -> p (b i)"),
                                       start=True, stop=True, skip_group_check=True)
                mm.then_inc(side_filled, 1)

            def add_field(i, weights):
                return pe.matmul(side[:, 0, 0:P], weights, gsum[:, i, :], start=i == 0, stop=i == FIELDS - 1,
                                 skip_group_check=True)

            def contract_w2(bt, k, before):
                if k == 0:
                    pe.wait_ge(side_copied, before)
                pe.wait_ge(w2_loaded[k % W2_SLOTS], bt * (16 * F_LOADS // W2_SLOTS) + 16 * (k // W2_SLOTS + 1))
                for i in range(W2_I):
                    mm = add_field(k * W2_I + i, w2[:, k % W2_SLOTS, i, :])
                mm.then_inc(w2_free, 1)
                if k == F_LOADS - 1:
                    pe.drain().then_inc(side_filled, 1)

            pe.sem_inc(w2_free, W2_SLOTS)
            pe.wait_ge(w0_summed, N_Y - 1)
            for g in range(len(L0)):
                layer0(g, g, g % PROD, 0)
            pe.wait_ge(w1_lo_ready, W1_PARTS)
            pe.wait_ge(w1_raw_loaded, 16)
            pe.wait_ge(consts_loaded, 32)

            def chunk(bt, q, t):
                groups = groups_of(t)
                before = side_before(bt, q)
                loads = 0
                for g, (layer, c, a, j) in enumerate(groups):
                    if g == 0:
                        pe.wait_ge(h1_copied, t + 1)
                    if g == XCOL_AT:
                        if q >= 0:
                            pe.wait_ge(side_copied, before)
                        pe.wait_ge(xt_loaded, t * 16 + 16)
                        pe.sem_inc(pe_passed, 1)
                        for s in range(SUB):
                            mm = pe.transpose(side[:, 0, s * FIELDS:(s + 1) * FIELDS], xt[:, s * P:(s + 1) * P],
                                              ident[0:FIELDS, 0:FIELDS])
                        mm.then_inc(side_filled, 1)
                        before = before + 1
                    if q >= 0 and g == H2T_AT:
                        pe.wait_ge(h2_copied, t)
                        turn_h2(before)
                        before = before + 1
                    if q >= 0 and g in G_AT:
                        form_g(bt, q, G_AT.index(g), before)
                        before = before + 1
                    if q == 3 and g in F_AT:
                        contract_w2(bt, loads, before)
                        loads += 1
                    if layer == 0:
                        layer0(L0_AT.index(g), groups_before(t, g), prod_slot(q, g), q % 2)
                    else:
                        layer1(groups, q, t, g)

            each_chunk(pe, chunk)
            def add_part(m, part):
                rows_in = slice(0, DENSE if part == 3 else P)
                return pe.matmul(hid1_ps[m], wt1[rows_in, part, m * P:(m + 1) * P], dense if part == 3 else z[:, part, :],
                                 start=part == 0, stop=part == 2, skip_group_check=True)

            pe.wait_ge(top_loaded, 16 * 7)
            pe.wait_ge(z_summed, 2 * CHUNKS - 1)
            for m in range(2):
                add_part(m, 0)
                add_part(m, 3)
            pe.wait_ge(h2_copied, CHUNKS)
            tail = side_before(BLOCKS - 1, 2) + 4
            turn_h2(tail)
            for m in range(2, 4):
                add_part(m, 0)
            form_g(BLOCKS - 1, PER_BLOCK - 1, 0, tail + 1)
            for m in range(2, 4):
                add_part(m, 3)
            pe.wait_ge(z_summed, 2 * CHUNKS)
            add_part(0, 1)
            add_part(1, 1)
            form_g(BLOCKS - 1, PER_BLOCK - 1, 1, tail + 2)
            add_part(2, 1)
            add_part(3, 1)
            for k in range(W2_SLOTS):
                contract_w2(BLOCKS - 1, k, tail + 3)
            pe.wait_ge(w2_in_w0_loaded, 16)
            for i in range(len(W0_TILES)):
                add_field(W2_SLOTS * W2_I + i, w0[:, i, :])
            for k in range(W2_IN_PROD):
                pe.wait_ge(w2_in_prod_loaded[k], 16)
                for i in range(k * W2_PROD_I, (k + 1) * W2_PROD_I):
                    mm = add_field(W2_PROD_AT + i, w2_in_prod[:, i, :])
            mm.then_inc(side_filled, 1)
            pe.wait_ge(side_copied, tail + 4)
            for m in range(4):
                add_part(m, 2).then_inc(hid_done, 1)
            for m in range(2):
                for k in range(4):
                    pe.wait_ge(hid_copied, k + 1)
                    mm = pe.matmul(acc[:, m, :], wt2[:, k, m * P:(m + 1) * P], hid1[:, k, :], start=k == 0, stop=k == 3)
                mm.then_inc(hid_done, 1)
            for k in range(2):
                pe.wait_ge(hid_copied, 5 + k)
                mm = pe.matmul(side[0:1, 0, :], wt3[:, k:k + 1], hid2[:, k, :], start=k == 0, stop=k == 1)
            mm.then_inc(hid_done, 1)


def kernel(**inputs):
    import numpy as np
    import concourse.bacc as bacc
    from concourse.bass_utils import run_bass_kernel_spmd

    f = {k: np.ascontiguousarray(np.asarray(v)) for k, v in inputs.items()}
    tables = [f[f"tbl_{i}"] for i in range(FIELDS)]
    arrays = {"tables": np.concatenate(tables)}
    assert sum(len(x) for x in tables) < 2 ** 24
    first_row = np.cumsum([0] + [len(x) for x in tables[:-1]]).astype(np.int32).reshape(STEPS, STEP_F)
    arrays["table_rows"] = np.ascontiguousarray(np.repeat(first_row.T, SAMPLES, axis=0))
    by_step = f["ids"].reshape(CHUNKS, SAMPLES, STEPS, STEP_F).transpose(3, 1, 0, 2)
    arrays["ids_steps"] = np.ascontiguousarray(by_step.reshape(P, CHUNKS, STEPS))
    for name in ("W_top1", "W_top2"):
        arrays[name] = f[name]
    pairs0 = f["L0_rec_W0"].reshape(FIELDS, FIELDS, NF)
    there, other = [], []
    for c, a in W0_TILES:
        i, j = slice(a * XA, (a + 1) * XA), slice(c * RB, (c + 1) * RB)
        there.append(pairs0[i, j].reshape(P, NF))
        if (c, a) in W0_BACK:
            other.append(pairs0[j, i].transpose(1, 0, 2).reshape(P, NF))
    arrays["w0_tiles"] = np.ascontiguousarray(np.stack(there, 1))
    arrays["w0_back"] = np.ascontiguousarray(np.concatenate(other, 1))
    pairs1 = f["L0_rec_W1"].reshape(N_X, XA, N_H, RB, NF)
    w1_tiles = pairs1.transpose(1, 3, 2, 0, 4).reshape(P, N_H, N_X, NF)
    arrays["w1_split"] = np.ascontiguousarray(np.concatenate([w1_tiles[:, c, a] for c, a in W1_SPLIT], 1))
    arrays["w1_raw"] = np.ascontiguousarray(np.stack([w1_tiles[:, c, a] for c, a in W1_RAW], 1))
    arrays["w2_rows"] = np.ascontiguousarray(f["L0_rec_W2"].reshape(FIELDS, NF, NF).transpose(1, 0, 2))
    arrays["w_top3_cols"] = np.ascontiguousarray(f["W_top3"].reshape(2, P).T)
    arrays["b_top1_cols"] = np.ascontiguousarray(f["b_top1"].reshape(4, P).T)
    arrays["b_top2_cols"] = np.ascontiguousarray(f["b_top2"].reshape(2, P).T)
    arrays["dense_rows"] = np.ascontiguousarray(f["dense_ctx"].T)
    arrays["identity"] = np.eye(P, dtype=np.float32)
    arrays["sample_mask"] = np.ascontiguousarray(np.tile(np.kron(np.eye(HALF_B), np.ones((DIM, 1))), (2, 1)).astype(np.float32))

    nc = bacc.Bacc("TRN2", target_bir_lowering=False, num_devices=1)
    ins = {k: nc.dram_tensor(k, a.shape, mybir.dt.from_np(a.dtype), kind="ExternalInput").ap() for k, a in arrays.items()}
    out = nc.dram_tensor("out", (BATCH, 1), F32, kind="ExternalOutput").ap()
    build(nc, ins, out)
    r = run_bass_kernel_spmd(nc, [arrays], core_ids=[0])
    return r.results[0]["out"]
```
